# Optimizing a Trainium2 kernel written in Bass

```python
import numpy as np
import jax
import jax.numpy as jnp

def _softmax(x, axis=-1):
    return jax.nn.softmax(x, axis=axis)

def _gelu(x):
    return jax.nn.gelu(x, approximate=True)

def _silu(x):
    return jax.nn.silu(x)

def _sigmoid(x):
    return jax.nn.sigmoid(x)

def _layernorm(x, axis=-1, eps=1e-05):
    m = jnp.mean(x, axis=axis, keepdims=True)
    v = jnp.var(x, axis=axis, keepdims=True)
    return (x - m) / jnp.sqrt(v + eps)

def _scatter_add(tgt, idx, src, axis=0):
    return tgt.at[idx].add(src)

def _segment_sum(src, seg, n):
    return jax.ops.segment_sum(src, seg, n)
kernel_name = 'mk_xattn_ffn_d1_seqx_r4_a761ad'

def setup_inputs(seed: int=0):
    np.random.seed(seed)
    _w = jnp.asarray

    def _rec_inputs():
        import jax
        import jax.numpy as jnp
        _rk = jax.random.key(seed)
        x = 0.0001212 + 1 * jax.random.normal(jax.random.fold_in(_rk, 1), (16, 128, 512), jnp.float32)
        _lenS = 128 - jax.random.randint(jax.random.fold_in(_rk, 7), (16,), 0, max(1, 128 // 4) + 1, jnp.int32)
        _lenS2 = 128 - jax.random.randint(jax.random.fold_in(_rk, 8), (16,), 0, max(1, 128 // 4) + 1, jnp.int32)
        _ctx_2048P = jax.random.normal(jax.random.fold_in(_rk, 11), (16, 16, 512), jnp.float32)
        _ctx_2048c = jax.random.dirichlet(jax.random.fold_in(_rk, 511), 0.3 * jnp.ones((16,), jnp.float32), (16, 128))
        _ctx_2048t = jnp.einsum('bsk,bkd->bsd', _ctx_2048c, _ctx_2048P)
        _ctx_2048t = _ctx_2048t * jax.lax.rsqrt(jnp.mean(jnp.square(_ctx_2048t)) + 1e-12) * 0.953939
        ctx_2048 = 0.000173663 + 1.0001 * (_ctx_2048t + 0.3 * jax.random.normal(jax.random.fold_in(_rk, 611), (16, 128, 512), jnp.float32))
        return (x, ctx_2048)
    x, ctx_2048 = _rec_inputs()

    def _L0_xattn_setup():
        import jax, jax.numpy as jnp
        import numpy as np
        B_DIM, T_DIM, C_DIM = (16, 256, 512)

        def _wkv(w, u, k, v):
            Bn, Tn, Cn = k.shape
            NEG_INF = jnp.float32(-1e+38)

            def step(carry, kv_t):
                p, q, o = carry
                kt, vt = kv_t
                no = jnp.maximum(o, u + kt)
                A = jnp.exp(o - no)
                E = jnp.exp(u + kt - no)
                y = (A * p + E * vt) / (A * q + E)
                no2 = jnp.maximum(w + o, kt)
                A2 = jnp.exp(w + o - no2)
                E2 = jnp.exp(kt - no2)
                return ((A2 * p + E2 * vt, A2 * q + E2, no2), y)
            init = (jnp.zeros((Bn, Cn), k.dtype), jnp.zeros((Bn, Cn), k.dtype), jnp.full((Bn, Cn), NEG_INF, k.dtype))
            kT = jnp.moveaxis(k, 1, 0)
            vT = jnp.moveaxis(v, 1, 0)
            _, yT = jax.lax.scan(step, init, (kT, vT))
            return jnp.moveaxis(yT, 0, 1)
        key = jax.random.key(seed)
        k1, k2, k3, k4 = jax.random.split(key, 4)
        w = -jnp.exp(jax.random.normal(k1, (C_DIM,), jnp.float32))
        u = jax.random.normal(k2, (C_DIM,), jnp.float32)
        k = jax.random.normal(k3, (B_DIM, T_DIM, C_DIM), jnp.float32)
        v = jax.random.normal(k4, (B_DIM, T_DIM, C_DIM), jnp.float32)
        return {'B': B_DIM, 'T': T_DIM, 'C': C_DIM, 'w': w, 'u': u, 'k': k, 'v': v}
    _L0_xattn_all = _L0_xattn_setup()
    _L0_xattn_in = {k: v for k, v in _L0_xattn_all.items() if k in ('w', 'u')}
    del _L0_xattn_all

    def _L0_ffn_setup():
        import jax, jax.numpy as jnp
        import numpy as np
        B, S, H = (2, 1024, 512)
        E, TOP_K = (8, 2)
        I_EXP, I_SHARED = (256, 1024)
        key = jax.random.key(seed)
        ks = jax.random.split(key, 9)
        sc = 0.02
        return {'hidden_states': jax.random.normal(ks[0], (B, S, H), jnp.float32), 'gate_w': jax.random.normal(ks[1], (E, H), jnp.float32) * sc, 'expert_gate_w': jax.random.normal(ks[2], (E, I_EXP, H), jnp.float32) * sc, 'expert_up_w': jax.random.normal(ks[3], (E, I_EXP, H), jnp.float32) * sc, 'expert_down_w': jax.random.normal(ks[4], (E, H, I_EXP), jnp.float32) * sc, 'shared_gate_w': jax.random.normal(ks[5], (I_SHARED, H), jnp.float32) * sc, 'shared_up_w': jax.random.normal(ks[6], (I_SHARED, H), jnp.float32) * sc, 'shared_down_w': jax.random.normal(ks[7], (H, I_SHARED), jnp.float32) * sc, 'shared_expert_gate_w': jax.random.normal(ks[8], (1, H), jnp.float32) * sc}
    _L0_ffn_all = _L0_ffn_setup()
    _L0_ffn_in = {k: v for k, v in _L0_ffn_all.items() if k in ('gate_w', 'expert_gate_w', 'expert_up_w', 'expert_down_w', 'shared_gate_w', 'shared_up_w', 'shared_down_w', 'shared_expert_gate_w')}
    del _L0_ffn_all
    return {'x': x, 'ctx_2048': ctx_2048, 'L0_xattn_w': _L0_xattn_in['w'], 'L0_xattn_u': _L0_xattn_in['u'], 'L0_ffn_gate_w': _L0_ffn_in['gate_w'], 'L0_ffn_expert_gate_w': _L0_ffn_in['expert_gate_w'], 'L0_ffn_expert_up_w': _L0_ffn_in['expert_up_w'], 'L0_ffn_expert_down_w': _L0_ffn_in['expert_down_w'], 'L0_ffn_shared_gate_w': _L0_ffn_in['shared_gate_w'], 'L0_ffn_shared_up_w': _L0_ffn_in['shared_up_w'], 'L0_ffn_shared_down_w': _L0_ffn_in['shared_down_w'], 'L0_ffn_shared_expert_gate_w': _L0_ffn_in['shared_expert_gate_w']}

def reference(x, ctx_2048, L0_xattn_w, L0_xattn_u, L0_ffn_gate_w, L0_ffn_expert_gate_w, L0_ffn_expert_up_w, L0_ffn_expert_down_w, L0_ffn_shared_gate_w, L0_ffn_shared_up_w, L0_ffn_shared_down_w, L0_ffn_shared_expert_gate_w):
    import jax
    import jax.numpy as jnp

    def _L0_xattn_ref(B, T, C, w, u, k, v):
        import jax, jax.numpy as jnp
        import numpy as np
        B_DIM, T_DIM, C_DIM = (16, 256, 512)

        def _wkv(w, u, k, v):
            Bn, Tn, Cn = k.shape
            NEG_INF = jnp.float32(-1e+38)

            def step(carry, kv_t):
                p, q, o = carry
                kt, vt = kv_t
                no = jnp.maximum(o, u + kt)
                A = jnp.exp(o - no)
                E = jnp.exp(u + kt - no)
                y = (A * p + E * vt) / (A * q + E)
                no2 = jnp.maximum(w + o, kt)
                A2 = jnp.exp(w + o - no2)
                E2 = jnp.exp(kt - no2)
                return ((A2 * p + E2 * vt, A2 * q + E2, no2), y)
            init = (jnp.zeros((Bn, Cn), k.dtype), jnp.zeros((Bn, Cn), k.dtype), jnp.full((Bn, Cn), NEG_INF, k.dtype))
            kT = jnp.moveaxis(k, 1, 0)
            vT = jnp.moveaxis(v, 1, 0)
            _, yT = jax.lax.scan(step, init, (kT, vT))
            return jnp.moveaxis(yT, 0, 1)
        return _wkv(w, u, k, v)

    def _L0_ffn_ref(hidden_states, gate_w, expert_gate_w, expert_up_w, expert_down_w, shared_gate_w, shared_up_w, shared_down_w, shared_expert_gate_w):
        import jax, jax.numpy as jnp
        import numpy as np
        B, S, H = (2, 1024, 512)
        E, TOP_K = (8, 2)
        I_EXP, I_SHARED = (256, 1024)
        b, s, h = hidden_states.shape
        x = hidden_states.reshape(-1, h)
        T = x.shape[0]
        n_experts = gate_w.shape[0]
        router_logits = x @ gate_w.T
        probs = jax.nn.softmax(router_logits.astype(jnp.float32), axis=-1)
        routing_weights, selected = jax.lax.top_k(probs, TOP_K)
        routing_weights = routing_weights.astype(x.dtype)
        comb = jnp.zeros((T, n_experts), x.dtype).at[jnp.arange(T)[:, None], selected].add(routing_weights)
        g = jnp.einsum('th,eih->tei', x, expert_gate_w)
        u = jnp.einsum('th,eih->tei', x, expert_up_w)
        expert_out = jnp.einsum('tei,ehi->teh', jax.nn.silu(g) * u, expert_down_w)
        moe_out = jnp.einsum('te,teh->th', comb, expert_out)
        sh = jax.nn.silu(x @ shared_gate_w.T) * (x @ shared_up_w.T) @ shared_down_w.T
        sh = jax.nn.sigmoid(x @ shared_expert_gate_w.T) * sh
        return (moe_out + sh).reshape(b, s, h)
    x = x + _L0_xattn_ref(16, 128, 512, L0_xattn_w, L0_xattn_u, _layernorm(x, axis=-1), ctx_2048)
    x = x + _L0_ffn_ref(_layernorm(x, axis=-1), L0_ffn_gate_w, L0_ffn_expert_gate_w, L0_ffn_expert_up_w, L0_ffn_expert_down_w, L0_ffn_shared_gate_w, L0_ffn_shared_up_w, L0_ffn_shared_down_w, L0_ffn_shared_expert_gate_w)
    return x

_drawn_inputs = setup_inputs


def setup_inputs(seed=0):
    import zlib

    import numpy as np

    out = dict(_drawn_inputs(seed))
    spreads = {}
    factors = {'L0_ffn_gate_w': 8.0,
     'L0_ffn_expert_gate_w': 7.185,
     'L0_ffn_expert_up_w': 7.083,
     'L0_ffn_expert_down_w': 7.066,
     'L0_ffn_shared_expert_gate_w': 64.0,
     'L0_ffn_shared_gate_w': 8.0,
     'L0_ffn_shared_up_w': 8.0,
     'L0_ffn_shared_down_w': 8.0}
    for name, (base, spread) in spreads.items():
        noise = np.random.default_rng([zlib.crc32(name.encode()), seed]).standard_normal(out[name].shape)
        drawn = base * np.exp(spread * noise) if base else spread * noise
        out[name] = jnp.asarray(drawn.astype(out[name].dtype))
    for name, factor in factors.items():
        out[name] = (out[name] * factor).astype(out[name].dtype)
    return out
```

```python
from contextlib import ExitStack

import concourse.bass as bass
from concourse import mybir

F32, F16, I32, U32 = mybir.dt.float32, mybir.dt.float16, mybir.dt.int32, mybir.dt.uint32
ALU, ACT, AX = mybir.AluOpType, mybir.ActivationFunctionType, mybir.AxisListType
ds = bass.ds

P = 128
B, T, H = 16, 128, 512
E, IE, IS, TOPK = 8, 256, 1024, 2
HC = H // P
IC = IE // P
SU = IS // IE
NSLOT = (TOPK * B * T + E * (P - 1)) // P
GUW, DW = HC * 2 * IE, IC * H
UW = GUW + DW
LAG = 5
NX = LAG + 1
SH1 = 13
SPLIT0 = 3
XS = 1024.0
EPS = 1e-5
RN = E + 1
SHARED, ROUTER = E, E + 1
S_GU, S_D, TANH, KAPPA, YINV = range(5)
HI_LO = [(0, 0), (0, 1), (1, 0)]
WKV0 = E * UW
SH0 = WKV0 + 4 * 2 * H
N_EXP = SU * SH1
N_TAIL = N_EXP + NSLOT
COMB1, COMB2 = 6, 12
TOP_STEPS, GATE_STEPS, NORM_STEPS, SCALE_STEPS = 5, 1, 4, 10
CONSTS, WKVC = 12, 6
RT_EXP, RT_MASK = 2, 5


def wait_from(eng, sem, value):
    if not (isinstance(value, int) and value <= 0):
        eng.wait_ge(sem, value)


def span(ap, start, n):
    return ap[:, start:start + n] if isinstance(start, int) else ap[:, ds(start, n)]


def rows(dram, t):
    return dram[t * P:(t + 1) * P, :] if isinstance(t, int) else dram[ds(t * P, P), :]


def turns(eng, turn):
    for i in range(SPLIT0):
        turn(i)
    turn(SPLIT0, shared_split=0)
    turn(SPLIT0 + 1, shared_split=2)
    turn(LAG, j=0, e=0)
    with eng.Fori(LAG + 1, LAG + E - 1) as i:
        turn(i, j=i - LAG, e=i - LAG)
    with eng.Fori(LAG + E - 1, B - 1) as i:
        turn(i, j=i - LAG)
    turn(B - 1, j=B - 1 - LAG)


class Link:

    def __init__(self, eng, sem):
        self.eng, self.sem, self.n = eng, sem, 0

    def __call__(self, ins):
        self.n += 1
        ins.then_inc(self.sem, 1)
        self.eng.wait_ge(self.sem, self.n)


def build(nc, x, ctx_t, wu, wr, wgu, wd, out):
    ctx = ExitStack()
    with ctx:
        def sb(name, shape, dt=F32):
            return ctx.enter_context(nc.sbuf_tensor(name, shape, dt))

        def bank(name):
            return ctx.enter_context(nc.psum_tensor(name, [P, 512], F32))

        def sems(names):
            return [ctx.enter_context(nc.semaphore(n)) for n in names.split()]

        x1_dram = nc.dram_tensor("x1_rows", (B * T, H), F32).ap()
        xn_dram = nc.dram_tensor("xn_rows", (B * T, H), F32).ap()
        acc_dram = nc.dram_tensor("acc_rows", (B * T, H), F32).ap()
        y_dram = nc.dram_tensor("expert_rows", (NSLOT * P, H), F32).ap()
        ids_dram = nc.dram_tensor("slot_tokens", (NSLOT * P, 1), I32).ap()

        wall = sb("wall", [P, SH0 + SU * UW])
        wall16 = wall[:, :].bitcast(F16)
        xt = sb("xt", [P, NX * 2 * H], F16)
        xb, cb = sb("xb", [P, 2 * H]), sb("cb", [P, 2 * H])
        kb, yb, xnb = sb("kb", [P, H]), sb("yb", [P, H]), sb("xnb", [P, H])
        growth, decay = sb("growth", [P, HC * T]), sb("decay", [P, HC * T])
        th = [sb(f"th{i}", [P, IE]) for i in range(2)]
        hb = [sb(f"hb{i}", [P, IE]) for i in range(2)]
        hx = [sb(f"hx{i}", [P, 2 * IE], F16) for i in range(2)]
        sb1 = sb("sb1", [P, 2 * H])
        ident, ones, tri = sb("ident", [P, P]), sb("ones", [P, P]), sb("tri", [P, P])
        wkvc, wu_sb = sb("wkvc", [P, 8, HC]), sb("wu_sb", [P, 2 * HC])
        wr_raw, wr_hl = sb("wr_raw", [P, HC * RN]), sb("wr_hl", [P, 2, HC * RN], F16)
        st6, mv, nrm = sb("st6", [P, 2, 6]), sb("mv", [P, 2, 2]), sb("nrm", [P, 2, 4])
        mhalf, warm = sb("mhalf", [P, 1]), sb("warm", [P, 1])
        ssq, scw, scf, sci = sb("ssq", [P, 2 * SU]), sb("scw", [P, 2]), sb("scf", [P, 9]), sb("sci", [P, 9], I32)
        scl = sb("scl", [P, (E + 2) * 5])
        lgt, mx8, ix8 = sb("lgt", [P, RN]), sb("mx8", [P, 8]), sb("ix8", [P, 8], U32)
        sg = sb("sg", [P, 1])
        lga, mxa, ixa = sb("lga", [P, B * E]), sb("mxa", [P, B * TOPK]), sb("ixa", [P, B * TOPK])
        gate, w12 = sb("gate", [P, B]), sb("w12", [P, TOPK, B])
        posi, toki = sb("posi", [P, TOPK, B], I32), sb("toki", [P, B], I32)
        eidi, idsi = sb("eidi", [P, NSLOT], I32), sb("idsi", [P, NSLOT], I32)
        idx = [sb(f"idx{i}", [P, 1], I32) for i in range(2)]

        iota8, iotaj, restart = sb("iota8", [P, E]), sb("iotaj", [P, NSLOT]), sb("restart", [P, E * B])
        gy = sb("gy", [P, 2])

        def taken(n, at=[0]):
            at[0] += n
            return cb[:, at[0] - n:at[0]]

        r_d, r_m, r_one0, r_one1, r_mask = taken(B * E), taken(B * TOPK), taken(B * E), taken(B * E), taken(B * E)
        r_tot, r_incl, r_pos, r_prod = growth[:, 0:128], growth[:, 128:256], growth[:, 256:384], growth[:, 384:512]
        r_sum, r_inv, r_posf = taken(B), taken(B), taken(TOPK * B)
        r_cnt, r_tiles, r_end, r_off = taken(E).bitcast(I32), taken(E), taken(E), taken(E)
        r_cmp, r_eid = taken(NSLOT * E), taken(NSLOT)
        ids_back, ids_float = yb[0:NSLOT, 0:P].bitcast(I32), yb[0:NSLOT, P:2 * P]

        xg = [xb[:, 0:H], xb[:, H:2 * H]]
        xe = [kb[:, :].bitcast(F16), xnb[:, :].bitcast(F16)]

        KT, YT, XT, LG = bank("KT"), bank("YT"), bank("XT"), bank("LG")
        GU = [bank("GU0"), bank("GU1")]
        HT, DN = bank("HT"), bank("DN")

        small_ld, x_ld, e_ld, s1_ld = sems("small_ld x_ld e_ld s1_ld")
        sh_ld = sems("sh_ld0 sh_ld1 sh_ld2 sh_ld3")
        x1_st, xn_st, acc_st, y_st, out_st = sems("x1_st xn_st acc_st y_st out_st")
        consts, tables, tables_act = sems("consts tables tables_act")
        stat1, agg1, norm1, k_rdy, k_t, kp1, kp2, exps, v1, v2 = sems(
            "stat1 agg1 norm1 k_rdy k_t kp1 kp2 exps v1 v2")
        scans, nd, rcp, ymul, y_rdy, y_t, x1_rdy, stat2, agg2, norm2 = sems(
            "scans nd rcp ymul y_rdy y_t x1_rdy stat2 agg2 norm2")
        xn_rdy, xn_t, x_hi, x_lo, logits, lg_rdy, gate_tanh, top, gated = sems(
            "xn_rdy xn_t x_hi x_lo logits lg_rdy gate_tanh top gated")
        gu, tanh, a1, h_rdy, h_t, h_hi, h_lo, dn, dn_free = sems("gu tanh a1 h_rdy h_t h_hi h_lo dn dn_free")
        sq, sq_sum, sq_red, scale_step, w_hi, w_ws, w_lo = sems("sq sq_sum sq_red scale_step w_hi w_ws w_lo")
        rt, rt_exp, rt_sums, rt_pos, ids_zero, ids_zst, scattered, ids_ld, ids_f, ids_t, ids_rdy = sems(
            "rt rt_exp rt_sums rt_pos ids_zero ids_zst scattered ids_ld ids_f ids_t ids_rdy")
        gather = sems("gather0 gather1")
        idx_rdy, g_t, g_hi, g_lo, y_rdy_e = sems("idx_rdy g_t g_hi g_lo y_rdy_e")
        cgather, acc_ld = sems("cgather0 cgather1"), sems("acc_ld0 acc_ld1")
        comb1, comb2, wr_lo, gyr, waited = sems("comb1 comb2 wr_lo gyr waited")

        def wkv(t, r, n=1):
            if isinstance(t, int):
                return wall[:, WKV0 + ((t % 2) * 4 + r) * H:WKV0 + ((t % 2) * 4 + r + n) * H]
            return wall[:, ds((t % 2) * (4 * H) + (WKV0 + r * H), n * H)]

        def combine_row(t, r):
            a = WKV0 + ((t % 2) * 4 + r) * H
            return wall[:, a:a + H]

        def part(buf, t):
            return buf[:, (t % 2) * H:(t % 2 + 1) * H] if isinstance(t, int) else buf[:, ds((t % 2) * H, H)]

        def xt_row(t, lo):
            return span(xt, (t % NX) * (2 * H) + lo * H, H)

        def split(base, off, n):
            return wall16[:, 2 * base + off:2 * base + off + n] if isinstance(base, int) \
                else wall16[:, ds(base * 2 + off, n)]

        def gate_up(base, lo, c, n=1):
            return split(base, lo * GUW + c * 2 * IE, n * 2 * IE)

        def down(base, lo, c, n=1):
            return split(base, 2 * GUW + lo * DW + c * H, n * H)

        def scale(row, k):
            return span(scl, row * 5 + k, 1)

        def sh_base(s):
            return SH0 + s * UW

        def unit_no(j):
            return SU * j if not isinstance(j, int) or j < SH1 else N_TAIL + SU * (j - SH1)

        def sum_no(j):
            return j if not isinstance(j, int) or j < SH1 else j + NSLOT

        def plain(eng):
            eng.sem_inc(waited, 1)

        block = ctx.enter_context(nc.Block())

        @block.sync
        def _(sp):
            def load(t):
                wait_from(sp, y_rdy, t - 1)
                plain(sp)
                wait_from(sp, x_ld, t * 32)
                plain(sp)
                wait_from(sp, x1_st, (t - 1) * 16)
                plain(sp)
                sp.dma_start(part(xb, t), rows(x, t)).then_inc(x_ld, 16)
                sp.dma_start(part(cb, t), rows(ctx_t, t)).then_inc(x_ld, 16)

            def store_x1(t):
                sp.wait_ge(x1_rdy, t + 1)
                plain(sp)
                sp.dma_start(rows(x1_dram, t), part(xb, t)).then_inc(x1_st, 16)

            def store_xn(t):
                sp.wait_ge(xn_rdy, t + 1)
                plain(sp)
                sp.dma_start(rows(xn_dram, t), xnb[:]).then_inc(xn_st, 16)

            def load_x1(j):
                wait_from(sp, s1_ld, j * 16)
                plain(sp)
                sp.wait_ge(x1_st, (j + 1) * 16)
                plain(sp)
                wait_from(sp, acc_st, j * 16 if not isinstance(j, int) or j < SH1 else (j - 1) * 16)
                plain(sp)
                sp.dma_start(part(sb1, j), rows(x1_dram, j)).then_inc(s1_ld, 16)

            def store_acc(j):
                sp.wait_ge(dn_free, sum_no(j) + 1)
                plain(sp)
                sp.dma_start(rows(acc_dram, j), part(sb1, j)).then_inc(acc_st, 16)

            def load_expert(e):
                base = (e + 1) * UW
                wait_from(sp, e_ld, e * 32)
                plain(sp)
                sp.wait_ge(w_lo, SU + e)
                plain(sp)
                src = (wgu[e], wd[e]) if isinstance(e, int) else tuple(
                    w[ds(e, 1), :, :].rearrange("a p n -> (a p) n") for w in (wgu, wd))
                sp.dma_start(span(wall, base, GUW), src[0]).then_inc(e_ld, 16)
                sp.dma_start(span(wall, base + GUW, DW), src[1]).then_inc(e_ld, 16)

            sp.dma_start(wu_sb[:], wu).then_inc(small_ld, 16)
            sp.dma_start(wr_raw[:], wr).then_inc(small_ld, 16)
            load(0)
            for s in range(SU):
                sp.dma_start(span(wall, (4 + s) * UW, GUW), wgu[E + s]).then_inc(sh_ld[s], 16)
                sp.dma_start(span(wall, (4 + s) * UW + GUW, DW), wd[E + s]).then_inc(sh_ld[s], 16)
                if s == 0:
                    load(1)
            sp.wait_ge(ids_zero, 1)
            sp.dma_start(ids_dram.rearrange("(j p) a -> j (p a)", p=P),
                         yb[0:NSLOT, 0:P].bitcast(I32)).then_inc(ids_zst, 16)

            def turn(i, j=None, e=None, shared_split=None):
                if e is not None:
                    load_expert(e)
                if j is not None:
                    if not (isinstance(j, int) and j == 0):
                        store_acc(j - 1)
                    load_x1(j)
                if not (isinstance(i, int) and i == 0):
                    store_x1(i - 1)
                    store_xn(i - 1)
                    if not (isinstance(i, int) and i == B - 1):
                        load(i + 1)

            turns(sp, turn)
            store_acc(B - LAG - 1)
            store_x1(B - 1)
            store_xn(B - 1)
            load_x1(B - LAG)
            sp.wait_ge(y_rdy, B)
            load_expert(E - 1)
            for j in range(B - LAG, SH1):
                if j > B - LAG:
                    store_acc(j - 1)
                    load_x1(j)
            sp.wait_ge(scattered, TOPK * B * 16)
            sp.wait_ge(rt_pos, 1)
            sp.dma_start(ids_back, ids_dram.rearrange("(j p) a -> j (p a)", p=P)).then_inc(ids_ld, 16)
            store_acc(SH1 - 1)

            def store_y(j):
                wait_from(sp, y_st, j * 16)
                plain(sp)
                sp.wait_ge(dn_free, j + (SH1 + 1))
                plain(sp)
                sp.dma_start(rows(y_dram, j), part(sb1, j)).then_inc(y_st, 16)

            store_y(0)
            with sp.Fori(1, NSLOT) as j:
                store_y(j)
            def load_acc(t):
                wait_from(sp, comb2, t - 1)
                sp.wait_ge(acc_st, 16 * (t + 1))
                sp.dma_start(combine_row(t, 0), rows(acc_dram, t)).then_inc(acc_ld[t % 2], 16)

            def store_out(t):
                sp.wait_ge(comb2, t + 1)
                sp.dma_start(rows(out, t), combine_row(t, 0)).then_inc(out_st, 16)
                if t + 2 < B:
                    sp.wait_ge(out_st, 16 * (t + 1))
                    load_acc(t + 2)

            sp.wait_ge(y_st, NSLOT * 16)
            load_x1(SH1)
            load_x1(SH1 + 1)
            sp.wait_ge(w_lo, SU + E)
            load_acc(0)
            load_acc(1)
            store_acc(SH1)
            load_x1(SH1 + 2)
            for t in range(COMB1):
                store_out(t)
            store_acc(SH1 + 1)
            for t in range(COMB1, COMB2):
                store_out(t)
            store_acc(SH1 + 2)
            for t in range(COMB2, B):
                store_out(t)
            sp.wait_ge(out_st, 16 * B)

        @block.gpsimd
        def _(pool):
            link = Link(pool, consts)
            pool.memset(yb[:].bitcast(I32), 0).then_inc(ids_zero, 1)
            link(pool.memset(ssq[:], 0.0))
            link(pool.memset(mhalf[:], -0.5))
            link(pool.memset(ones[:], 1.0))
            link(pool.memset(ident[:], 0.0))
            link(pool.affine_select(out=ident[:], in_=ident[:], compare_op=ALU.not_equal, fill=1.0,
                                    base=0, pattern=[[-1, P]], channel_multiplier=1))
            link(pool.affine_select(out=tri[:], in_=ones[:], compare_op=ALU.is_gt, fill=0.0,
                                    base=0, pattern=[[1, P]], channel_multiplier=-1))
            link(pool.iota(decay[:], [[0, HC], [1, T]], base=0, channel_multiplier=0,
                           allow_small_or_imprecise_dtypes=True))
            link(pool.iota(toki[:], [[P, B]], base=0, channel_multiplier=1))
            for buf, pattern in (iota8, [[1, E]]), (iotaj, [[1, NSLOT]]), (restart, [[0, E], [1, B]]):
                link(pool.iota(buf[:], pattern, base=0, channel_multiplier=0,
                               allow_small_or_imprecise_dtypes=True))
            link(pool.tensor_scalar(restart[:], restart[:], 1.0, None, ALU.min))
            assert link.n == CONSTS

            def norm(t, k, stats_rdy, steps, used):
                pool.wait_ge(stats_rdy, t + 1)
                wait_from(pool, used, t)
                plain(pool)
                nc.gpsimd.tensor_scalar(nrm[:, k, 0:1], mv[:, k, 1:2], EPS, None, ALU.add).then_inc(steps, 1)
                nc.gpsimd.tensor_scalar(nrm[:, k, 1:2], mv[:, k, 0:1], -1.0, None, ALU.mult).then_inc(steps, 1)
                pool.wait_ge(steps, t * NORM_STEPS + 2)
                nc.gpsimd.tensor_tensor(nrm[:, k, 2:3], nrm[:, k, 0:1], mhalf[:], ALU.pow).then_inc(steps, 1)
                pool.wait_ge(steps, t * NORM_STEPS + 3)
                nc.gpsimd.tensor_tensor(nrm[:, k, 3:4], nrm[:, k, 1:2], nrm[:, k, 2:3], ALU.mult).then_inc(steps, 1)

            def second_exponent(t):
                pool.wait_ge(kp1, t + 1)
                nc.gpsimd.tensor_tensor(wkv(t, 2).rearrange("p (c t) -> p c t", c=HC),
                                        wkv(t, 0).rearrange("p (c t) -> p c t", c=HC),
                                        wkvc[:, 4, :].unsqueeze(2).to_broadcast([P, HC, T]), ALU.add).then_inc(kp2, 1)

            def second_product(t):
                pool.wait_ge(exps, t + 1)
                nc.gpsimd.tensor_tensor(wkv(t, 3), wkv(t, 2), part(cb, t), ALU.mult).then_inc(v2, 1)

            def expert_lo(e):
                pool.wait_ge(w_ws, 2 * e + 2)
                raw = (e + 1) * UW
                half = GUW // 2
                for k in range(2):
                    nc.gpsimd.tensor_tensor(split(e * UW, GUW + k * half, half), span(wall, raw + k * half, half),
                                            split(e * UW, k * half, half), ALU.subtract)
                nc.gpsimd.tensor_tensor(down(e * UW, 1, 0, IC), span(wall, raw + GUW, DW), down(e * UW, 0, 0, IC),
                                        ALU.subtract).then_inc(w_lo, 1)

            norm(0, 0, agg1, norm1, k_rdy)
            pool.wait_ge(tables, WKVC)

            def turn(i, j=None, e=None, shared_split=None):
                second_exponent(i)
                if not (isinstance(i, int) and i == 0):
                    norm(i - 1, 1, agg2, norm2, xn_rdy)
                second_product(i)
                if not (isinstance(i, int) and i == B - 1):
                    norm(i + 1, 0, agg1, norm1, k_rdy)
                if e is not None:
                    expert_lo(e)

            turns(pool, turn)
            norm(B - 1, 1, agg2, norm2, xn_rdy)
            expert_lo(E - 1)

            pool.wait_ge(ids_zst, 16)
            pool.wait_ge(rt_pos, 1)
            for t in range(B):
                for k in range(TOPK):
                    pool.indirect_dma_start(ids_dram, bass.IndirectOffsetOnAxis(ap=posi[:, k, t:t + 1], axis=0),
                                            toki[:, t:t + 1], None).then_inc(scattered, 16)

            pool.wait_ge(ids_rdy, 1)
            pool.wait_ge(xn_st, 16 * B)

            def gather_tile(j, r):
                wait_from(pool, gather[r], (j - 2) // 2 * 16 + 16 if isinstance(j, int) else 16 * ((j - r) // 2))
                pool.tensor_copy(idx[r][:], span(idsi, j, 1)).then_inc(idx_rdy, 1)
                wait_from(pool, g_t, j - 1)
                pool.wait_ge(idx_rdy, j + 1)
                plain(pool)
                pool.indirect_dma_start(xg[r], None, xn_dram, bass.IndirectOffsetOnAxis(ap=idx[r][:, 0:1], axis=0)
                                        ).then_inc(gather[r], 16)

            gather_tile(0, 0)
            gather_tile(1, 1)
            with pool.Fori(1, NSLOT // 2) as m:
                gather_tile(m * 2, 0)
                gather_tile(m * 2 + 1, 1)
            for j in range(NSLOT // 2 * 2, NSLOT):
                gather_tile(j, j % 2)

            pool.wait_ge(w_lo, SU + E)
            pool.wait_ge(y_st, NSLOT * 16)
            for t in range(B):
                wait_from(pool, comb2, t - 1)
                for k in range(TOPK):
                    pool.indirect_dma_start(combine_row(t, 1 + k), None, y_dram,
                                            bass.IndirectOffsetOnAxis(ap=posi[:, k, t:t + 1], axis=0)
                                            ).then_inc(cgather[t % 2], 16)
                if t >= 1:
                    pool.wait_ge(cgather[(t - 1) % 2], 32 * ((t - 1) // 2 + 1))

        @block.scalar
        def _(act):
            def square(src, junk, n, out1):
                nc.scalar.activation(junk, src, ACT.Square, accum_out=out1).then_inc(sq, 1)

            act.wait_ge(consts, CONSTS)
            nc.scalar.activation(warm[:], mhalf[:], ACT.Tanh).then_inc(tables_act, 1)
            act.wait_ge(tables, WKVC)
            nc.scalar.activation(wkvc[:, 6, :], wkvc[:, 5, :], ACT.Exp).then_inc(tables_act, 1)
            act.wait_ge(small_ld, 32)
            square(wr_raw[:], growth[:, 0:HC * RN], HC * RN, ssq[:, 0:1])

            def first_norm(t):
                act.wait_ge(norm1, (t + 1) * NORM_STEPS)
                wait_from(act, k_t, t)
                plain(act)
                nc.scalar.activation(kb[:], part(xb, t), ACT.Identity, bias=nrm[:, 0, 3:4],
                                     scale=nrm[:, 0, 2:3]).then_inc(k_rdy, 1)

            def second_norm(t):
                act.wait_ge(norm2, (t + 1) * NORM_STEPS)
                wait_from(act, xn_t, t)
                wait_from(act, xn_st, 16 * t)
                plain(act)
                nc.scalar.activation(xnb[:], part(xb, t), ACT.Identity, bias=nrm[:, 1, 3:4],
                                     scale=nrm[:, 1, 2:3]).then_inc(xn_rdy, 1)

            def both_exps(t):
                act.wait_ge(kp2, t + 1)
                rows2 = wkv(t, 0, 4).rearrange("p (a n) -> p a n", a=2)[:, :, 0:H]
                plain(act)
                nc.scalar.activation(rows2, rows2, ACT.Exp).then_inc(exps, 1)

            def act_hi(t):
                act.wait_ge(xn_t, t + 1)
                plain(act)
                nc.scalar.activation(xt_row(t, 0), XT[:], ACT.Copy, scale=XS).then_inc(x_hi, 1)

            def router_out(t):
                act.wait_ge(logits, t + 1)
                wait_from(act, top, t * TOP_STEPS)
                nc.scalar.activation(lgt[:], LG[:, 0:RN], ACT.Copy, scale=scale(ROUTER, YINV)).then_inc(lg_rdy, 1)
                act.wait_ge(lg_rdy, t + 1)
                wait_from(act, gated, t * GATE_STEPS)
                nc.scalar.activation(sg[:], lgt[:, E:E + 1], ACT.Tanh, scale=0.5).then_inc(gate_tanh, 1)

            def unit_tanh(n, par, row):
                act.wait_ge(gu, n + 1)
                wait_from(act, h_rdy, n - 1)
                plain(act)
                nc.scalar.activation(th[par][:], GU[par][:, 0:IE], ACT.Tanh, scale=scale(row, TANH)).then_inc(tanh, 1)

            def unit_hi(n, par):
                act.wait_ge(h_t, n + 1)
                wait_from(act, dn, n - 1)
                nc.scalar.activation(hx[par][:, 0:IE], HT[:, 0:IE], ACT.Copy).then_inc(h_hi, 1)

            def shared_square(s):
                act.wait_ge(sh_ld[s], 32)
                wait_from(act, sq_sum, 1)
                raw = (4 + s) * UW
                square(span(wall, raw, GUW), span(wall, s * UW, GUW), GUW, ssq[:, s:s + 1])
                square(span(wall, raw + GUW, DW), span(wall, s * UW + GUW, DW), DW, ssq[:, SU + s:SU + s + 1])

            def shared_hi(s):
                raw = (4 + s) * UW
                act.wait_ge(scale_step, 2 * SCALE_STEPS + 1)
                nc.scalar.activation(gate_up(sh_base(s), 0, 0, HC), span(wall, raw, GUW), ACT.Copy,
                                     scale=scale(SHARED, S_GU)).then_inc(w_hi, 1)
                nc.scalar.activation(down(sh_base(s), 0, 0, IC), span(wall, raw + GUW, DW), ACT.Copy,
                                     scale=scale(SHARED, S_D)).then_inc(w_hi, 1)

            def expert_square(e, k):
                raw = (e + 1) * UW
                if k == 0:
                    act.wait_ge(e_ld, (e + 1) * 32)
                    act.wait_ge(w_lo, SU + e)
                    act.wait_ge(sq_sum, e + 2)
                    plain(act)
                    square(span(wall, raw, GUW), span(wall, e * UW, GUW), GUW, ssq[:, 0:1])
                else:
                    square(span(wall, raw + GUW, DW), span(wall, e * UW + GUW, DW), DW, ssq[:, 1:2])

            def expert_hi(e):
                raw = (e + 1) * UW
                act.wait_ge(scale_step, (e + 3) * SCALE_STEPS + 1)
                plain(act)
                nc.scalar.activation(gate_up(e * UW, 0, 0, HC), span(wall, raw, GUW), ACT.Copy,
                                     scale=scale(e, S_GU)).then_inc(w_hi, 1)
                nc.scalar.activation(down(e * UW, 0, 0, IC), span(wall, raw + GUW, DW), ACT.Copy,
                                     scale=scale(e, S_D)).then_inc(w_hi, 1)
                act.wait_ge(w_hi, 2 * SU + 3 + 2 * e)
                plain(act)
                nc.scalar.activation(span(wall, raw, GUW), span(wall, raw, GUW), ACT.Copy,
                                     scale=scale(e, S_GU)).then_inc(w_ws, 1)
                nc.scalar.activation(span(wall, raw + GUW, DW), span(wall, raw + GUW, DW), ACT.Copy,
                                     scale=scale(e, S_D)).then_inc(w_ws, 1)

            first_norm(0)
            act.wait_ge(scale_step, SCALE_STEPS + 1)
            nc.scalar.activation(wr_hl[:, 0, :], wr_raw[:], ACT.Copy, scale=scale(ROUTER, S_GU)).then_inc(w_hi, 1)

            def turn(i, j=None, e=None, shared_split=None):
                is_first, is_last = isinstance(i, int) and i == 0, isinstance(i, int) and i == B - 1
                n = None if j is None else j * SU
                if n is not None and not (isinstance(j, int) and j == 0):
                    unit_hi(n - 1, 1)
                both_exps(i)
                if n is not None:
                    unit_tanh(n, 0, SHARED)
                if not is_first:
                    second_norm(i - 1)
                if n is not None:
                    unit_hi(n, 0)
                    if e is not None:
                        expert_square(e, 0)
                    unit_tanh(n + 1, 1, SHARED)
                if not is_first:
                    act_hi(i - 1)
                if n is not None:
                    unit_hi(n + 1, 1)
                    if e is not None:
                        expert_square(e, 1)
                    unit_tanh(n + 2, 0, SHARED)
                    unit_hi(n + 2, 0)
                if not is_last:
                    first_norm(i + 1)
                if not is_first:
                    router_out(i - 1)
                if n is not None:
                    unit_tanh(n + 3, 1, SHARED)
                if e is not None:
                    expert_hi(e)
                if is_first:
                    shared_square(0)
                    shared_square(1)
                if shared_split is not None:
                    if shared_split == 0:
                        shared_square(2)
                        shared_square(3)
                    shared_hi(shared_split)
                    shared_hi(shared_split + 1)

            turns(act, turn)

            def shared_tile(j, beside=lambda u: None):
                n, par = unit_no(j), unit_no(j) % 2
                unit_hi(n - 1, 1 - par)
                for u in range(SU):
                    unit_tanh(n + u, (par + u) % 2, SHARED)
                    beside(u)
                    if u < SU - 1:
                        unit_hi(n + u, (par + u) % 2)

            def last_of_mix(u):
                if u == 0:
                    second_norm(B - 1)
                if u == 1:
                    act_hi(B - 1)
                if u == 2:
                    router_out(B - 1)
                    expert_square(E - 1, 0)
                    expert_square(E - 1, 1)
                if u == 3:
                    expert_hi(E - 1)

            shared_tile(B - LAG, last_of_mix)

            def route_exps():
                act.wait_ge(rt, RT_EXP)
                nc.scalar.activation(r_d, r_d, ACT.Exp).then_inc(rt_exp, 1)
                nc.scalar.activation(r_m, r_m, ACT.Exp).then_inc(rt_exp, 1)

            route_exps()
            for j in range(B - LAG + 1, SH1):
                shared_tile(j)

            def gathered_hi(j, r):
                act.wait_ge(g_t, j + 1)
                wait_from(act, gu, N_EXP + j - 1)
                nc.scalar.activation(xe[r][:, 0:H], XT[:], ACT.Copy, scale=XS).then_inc(g_hi, 1)

            def expert_unit(j, r, ahead=True):
                e = act.value_load(span(eidi[0:1, :], j, 1), min_val=0, max_val=E - 1)
                unit_hi(N_EXP + j - 1, (N_EXP + 1 + r) % 2)
                if ahead:
                    gathered_hi(j + 1, 1 - r)
                unit_tanh(N_EXP + j, (N_EXP + r) % 2, e)

            act.wait_ge(rt_pos, 2)
            gathered_hi(0, 0)
            expert_unit(0, 0)
            with act.Fori(0, (NSLOT - 3) // 2) as m:
                expert_unit(m * 2 + 1, 1)
                expert_unit(m * 2 + 2, 0)
            expert_unit(NSLOT - 2, 1)
            expert_unit(NSLOT - 1, 0, ahead=False)
            for j in range(SH1, B):
                shared_tile(j)
            unit_hi(N_TAIL + SU * (B - SH1) - 1, (N_TAIL + 1) % 2)

        @block.tensor
        def _(pe):
            def transposes(dst, src, n, done):
                for c in range(n):
                    ins = nc.tensor.transpose(dst[:, c * P:(c + 1) * P], src[:, c * P:(c + 1) * P], ident[:])
                ins.then_inc(done, 1)

            def keys_t(t):
                pe.wait_ge(k_rdy, t + 1)
                wait_from(pe, kp1, t)
                transposes(KT, kb, HC, k_t)

            def y_back(t):
                pe.wait_ge(y_rdy, t + 1)
                wait_from(pe, x1_rdy, t)
                transposes(YT, yb, HC, y_t)

            def xn_t_(t):
                pe.wait_ge(xn_rdy, t + 1)
                wait_from(pe, x_lo, t)
                transposes(XT, xnb, HC, xn_t)

            def router(t):
                pe.wait_ge(x_lo, t + 1)
                if isinstance(t, int) and t == 0:
                    pe.wait_ge(wr_lo, 1)
                wait_from(pe, lg_rdy, t)
                for m in range(3 * HC):
                    c, (xp, wp) = m // 3, HI_LO[m % 3]
                    ins = nc.tensor.matmul(LG[:, 0:RN], span(xt, (t % NX) * (2 * H) + (xp * H + c * P), P),
                                           wr_hl[:, wp, c * RN:(c + 1) * RN], start=m == 0, stop=m == 3 * HC - 1)
                ins.then_inc(logits, 1)

            def sum_squares(k, squares, cols):
                pe.wait_ge(sq, squares)
                nc.tensor.matmul(YT[:, 0:cols], ones[:], ssq[:, 0:cols], start=True, stop=True).then_inc(sq_sum, 1)

            def products(par, lhs, base, first, last):
                for m in range(first, last):
                    c, (xp, wp) = m // 3, HI_LO[m % 3]
                    ins = nc.tensor.matmul(GU[par][:], lhs(xp, c), gate_up(base, wp, c), start=m == 0,
                                           stop=m == 3 * HC - 1)
                return ins

            def hidden_t(n, par):
                pe.wait_ge(h_rdy, n + 1)
                wait_from(pe, h_lo, n)
                transposes(HT, hb[par], IC, h_t)

            def down_products(n, par, base, start, stop, sums):
                pe.wait_ge(h_lo, n + 1)
                if start:
                    wait_from(pe, dn_free, sums)
                for m in range(3 * IC):
                    c, (hp, wp) = m // 3, HI_LO[m % 3]
                    ins = nc.tensor.matmul(DN[:], hx[par][:, hp * IE + c * P:hp * IE + (c + 1) * P],
                                           down(base, wp, c), start=start and m == 0, stop=stop and m == 3 * IC - 1)
                ins.then_inc(dn, 1)

            def unit(n, par, lhs, base, prev):
                wait_from(pe, h_rdy, n - 1)
                products(par, lhs, base, 0, 8)
                if prev is not None:
                    hidden_t(n - 1, 1 - par)
                products(par, lhs, base, 8, 3 * HC).then_inc(gu, 1)
                if prev is not None:
                    down_products(n - 1, 1 - par, *prev)

            def shared_down(j, u):
                return sh_base(u), u == 0, u == SU - 1, sum_no(j)

            def shared_lhs(j):
                return lambda xp, c: span(xt, (j % NX) * (2 * H) + (xp * H + c * P), P)

            def shared_units(j, prev, beside=lambda u: None):
                n = unit_no(j)
                par0 = n % 2 if isinstance(n, int) else 0
                for u in range(SU):
                    if isinstance(j, int) and j == 0:
                        pe.wait_ge(w_lo, u + 1)
                    unit(n + u, (par0 + u) % 2, shared_lhs(j), sh_base(u), prev)
                    prev = shared_down(j, u)
                    beside(u)

            pe.wait_ge(consts, CONSTS)
            sum_squares(0, 1, 2)
            keys_t(0)

            def turn(i, j=None, e=None, shared_split=None):
                is_first, is_last = isinstance(i, int) and i == 0, isinstance(i, int) and i == B - 1
                def sums():
                    if e is not None:
                        sum_squares(2 + e, 2 * SU + 3 + 2 * e, 2)
                    if shared_split == 0:
                        sum_squares(1, 2 * SU + 1, 2 * SU)
                def y_turn():
                    if e is not None:
                        pe.wait_ge(sq_red, e + 3)
                    if shared_split == 0:
                        pe.wait_ge(sq_red, 2)
                    if is_first:
                        pe.wait_ge(sq_red, 1)
                    y_back(i)
                if j is None:
                    if not is_first:
                        xn_t_(i - 1)
                        router(i - 1)
                    sums()
                    y_turn()
                    keys_t(i + 1)
                else:
                    prev = None if isinstance(j, int) and j == 0 else shared_down(j - 1, SU - 1)

                    def second_half(u):
                        if u == 1:
                            xn_t_(i - 1)
                        if u == 2:
                            router(i - 1)
                            sums()

                    shared_units(j, prev, second_half)
                    if not is_last:
                        keys_t(i + 1)
                    y_turn()

            turns(pe, turn)

            def last_of_mix(u):
                if u == 1:
                    xn_t_(B - 1)
                if u == 2:
                    router(B - 1)
                    sum_squares(1 + E, 2 * SU + 1 + 2 * E, 2)

            shared_units(B - LAG, shared_down(B - LAG - 1, SU - 1), last_of_mix)

            def route_sums(u):
                if u > 0:
                    return
                pe.wait_ge(rt, RT_MASK)
                nc.tensor.matmul(KT[:, 0:B * E], tri[:], r_mask, start=True, stop=True)
                nc.tensor.matmul(LG[:, 0:B * E], ones[:], r_mask, start=True, stop=True).then_inc(rt_sums, 1)

            def ids_back_t():
                pe.wait_ge(ids_f, 1)
                nc.tensor.transpose(KT[:, 0:NSLOT], ids_float, ident[0:NSLOT, 0:NSLOT]).then_inc(ids_t, 1)

            for j in range(B - LAG + 1, SH1):
                if j == B - LAG + 1:
                    shared_units(j, shared_down(j - 1, SU - 1), route_sums)
                else:
                    shared_units(j, shared_down(j - 1, SU - 1))
            ids_back_t()

            def gathered_t(j, r):
                pe.wait_ge(gather[r], 16 * (j // 2 + 1) if isinstance(j, int) else 16 * ((j - r) // 2 + 1))
                wait_from(pe, g_lo, j)
                transposes(XT, xg[r], HC, g_t)

            def expert_unit(j, r, prev_sum, ahead=True):
                e = pe.value_load(span(eidi[0:1, :], j, 1), min_val=0, max_val=E - 1)
                if isinstance(j, int) and j == 0:
                    prev = shared_down(SH1 - 1, SU - 1)
                else:
                    ep = pe.value_load(span(eidi[0:1, :], j - 1, 1), min_val=0, max_val=E - 1)
                    prev = (ep * UW, True, True, prev_sum)
                if ahead:
                    gathered_t(j + 1, 1 - r)
                pe.wait_ge(g_lo, j + 1)
                unit(N_EXP + j, (N_EXP + r) % 2, lambda xp, c: xe[r][:, xp * H + c * P:xp * H + (c + 1) * P],
                     e * UW, prev)
                return e

            pe.wait_ge(w_lo, SU + E)
            pe.wait_ge(rt_pos, 2)
            gathered_t(0, 0)
            expert_unit(0, 0, None)
            with pe.Fori(0, (NSLOT - 3) // 2) as m:
                expert_unit(m * 2 + 1, 1, m * 2 + SH1)
                expert_unit(m * 2 + 2, 0, m * 2 + (SH1 + 1))
            expert_unit(NSLOT - 2, 1, NSLOT - 3 + SH1)
            last_e = expert_unit(NSLOT - 1, 0, NSLOT - 2 + SH1, ahead=False)
            prev = (last_e * UW, True, True, NSLOT - 1 + SH1)
            for j in range(SH1, B):
                shared_units(j, prev)
                prev = shared_down(j, SU - 1)
            n = N_TAIL + SU * (B - SH1) - 1
            hidden_t(n, n % 2)
            down_products(n, n % 2, *prev)

        @block.vector
        def _(dve):
            TT, STT = nc.vector.tensor_tensor, nc.vector.scalar_tensor_tensor

            def grid(ap):
                return ap.rearrange("p (c t) -> p c t", t=T)

            def keys(t):
                dve.wait_ge(k_t, t + 1)
                wait_from(dve, ymul, t - 1)
                TT(wkv(t, 0), KT[:], growth[:], ALU.subtract).then_inc(kp1, 1)

            def scans_(t):
                dve.wait_ge(x_ld, t * 32 + 32)
                dve.wait_ge(exps, t + 1)
                TT(wkv(t, 1), wkv(t, 0), part(cb, t), ALU.mult).then_inc(v1, 1)
                dve.wait_ge(v1, t + 1)
                for r in range(2):
                    nc.vector.tensor_tensor_scan(wkv(t, r), decay[:], wkv(t, r), 0.0, ALU.mult,
                                                 ALU.add).then_inc(scans, 1)
                dve.wait_ge(scans, t * 2 + 2)
                dve.wait_ge(v2, t + 1)
                now, before = grid(wkv(t, 2, 2))[:, :, 1:T], grid(wkv(t, 0, 2))[:, :, 0:T - 1]
                TT(now, now, before, ALU.add).then_inc(nd, 1)

            def reciprocals(t, first):
                if first == 0:
                    dve.wait_ge(nd, t + 1)
                for c in range(first, first + 2):
                    a = wkv_chunk(t, 2, c)
                    nc.vector.reciprocal(a, a).then_inc(rcp, 1)

            def wkv_chunk(t, r, c):
                off = r * H + c * T
                if isinstance(t, int):
                    return wall[:, WKV0 + (t % 2) * 4 * H + off:WKV0 + (t % 2) * 4 * H + off + T]
                return wall[:, ds((t % 2) * (4 * H) + (WKV0 + off), T)]

            def quotient(t):
                dve.wait_ge(rcp, t * HC + HC)
                wait_from(dve, y_t, t)
                if isinstance(t, int) and t == 0:
                    dve.wait_ge(ids_zst, 16)
                TT(yb[:], wkv(t, 3), wkv(t, 2), ALU.mult).then_inc(ymul, 1)
                dve.wait_ge(ymul, t + 1)
                nc.vector.tensor_scalar(grid(yb[:])[:, :, 0:1], grid(part(cb, t))[:, :, 0:1], 1.0, None,
                                        ALU.mult).then_inc(y_rdy, 1)

            def stats(t, k, stat, agg, used):
                plain(dve)
                nc.vector.bn_stats(st6[:, k, :], part(xb, t)).then_inc(stat, 1)
                dve.wait_ge(stat, t + 1)
                wait_from(dve, used, t * NORM_STEPS)
                plain(dve)
                nc.vector.bn_aggr(mv[:, k, :], st6[:, k, :]).then_inc(agg, 1)

            def stats1(t):
                dve.wait_ge(x_ld, t * 32 + 32)
                stats(t, 0, stat1, agg1, norm1)

            def residual(t):
                dve.wait_ge(y_t, t + 1)
                TT(part(xb, t), YT[:], part(xb, t), ALU.add).then_inc(x1_rdy, 1)
                dve.wait_ge(x1_rdy, t + 1)
                stats(t, 1, stat2, agg2, norm2)

            def act_lo(t):
                dve.wait_ge(x_hi, t + 1)
                STT(xt_row(t, 1), XT[:], XS, xt_row(t, 0), ALU.mult, ALU.subtract).then_inc(x_lo, 1)

            def top2_gate(t):
                dve.wait_ge(lg_rdy, t + 1)
                plain(dve)
                nc.vector.max(mx8[:], lgt[:, 0:E]).then_inc(top, 1)
                dve.wait_ge(top, t * TOP_STEPS + 1)
                plain(dve)
                nc.vector.max_index(ix8[:], mx8[:], lgt[:, 0:E]).then_inc(top, 1)
                dve.wait_ge(gate_tanh, t + 1)
                nc.vector.tensor_scalar(span(gate, t, 1), sg[:], 0.5, 0.5, ALU.mult, ALU.add).then_inc(gated, 1)
                nc.vector.tensor_scalar(span(lga, t * E, E), lgt[:, 0:E], 1.0, None, ALU.mult).then_inc(top, 1)
                nc.vector.tensor_scalar(span(mxa, t * TOPK, TOPK), mx8[:, 0:TOPK], 1.0, None,
                                        ALU.mult).then_inc(top, 1)
                dve.wait_ge(top, t * TOP_STEPS + 2)
                nc.vector.tensor_scalar(span(ixa, t * TOPK, TOPK), ix8[:, 0:TOPK], 1.0, None,
                                        ALU.mult).then_inc(top, 1)

            def scales(k, row):
                base = 0 if isinstance(k, int) and k == 0 else k * SCALE_STEPS + 1
                n = 0

                def step(ins):
                    nonlocal n
                    n += 1
                    ins.then_inc(scale_step, 1)
                    dve.wait_ge(scale_step, base + n)

                dve.wait_ge(sq_sum, k + 1)
                if isinstance(row, int) and row == SHARED:
                    ins = nc.vector.tensor_reduce(scw[:], YT[:, 0:2 * SU].rearrange("p (a s) -> p a s", s=SU),
                                                  AX.X, ALU.max)
                else:
                    ins = nc.vector.tensor_copy(scw[:], YT[:, 0:2])
                ins.then_inc(sq_red, 1)
                dve.wait_ge(sq_red, k + 1)
                e2, h2, e_gu, h_gu, h_d = sci[:, 0:2], sci[:, 2:4], sci[:, 0:1], sci[:, 2:3], sci[:, 3:4]
                field = [sci[:, 4 + f:5 + f] for f in range(5)]
                TS = nc.vector.tensor_scalar
                step(TS(e2, scw[:].bitcast(I32), 23, None, ALU.logical_shift_right))
                step(TS(h2, e2, 1, None, ALU.add))
                step(TS(h2, h2, 1, None, ALU.logical_shift_right))
                step(TS(sci[:, 4:6], h2, -1, 205, ALU.mult, ALU.add))
                step(TS(field[TANH], h_gu, 38, None, ALU.add))
                step(STT(field[KAPPA], h_gu, 2, e_gu, ALU.mult, ALU.subtract))
                step(TS(field[KAPPA], field[KAPPA], 83, None, ALU.add))
                step(STT(field[YINV], e_gu, -84, h_d, ALU.add, ALU.add))
                step(TS(field[YINV], field[YINV], 0, 254, ALU.max, ALU.min))
                step(TS(span(scl, row * 5, 5).bitcast(I32), sci[:, 4:9], 23, None, ALU.logical_shift_left))
                assert n == SCALE_STEPS

            def shared_lo(s):
                raw, base = (4 + s) * UW, sh_base(s)
                dve.wait_ge(w_hi, 2 * s + 3)
                STT(gate_up(base, 1, 0, HC), span(wall, raw, GUW), scale(SHARED, S_GU), gate_up(base, 0, 0, HC),
                    ALU.mult, ALU.subtract)
                STT(down(base, 1, 0, IC), span(wall, raw + GUW, DW), scale(SHARED, S_D), down(base, 0, 0, IC),
                    ALU.mult, ALU.subtract).then_inc(w_lo, 1)

            def hidden(n, par, row):
                dve.wait_ge(tanh, n + 1)
                STT(th[par][:], th[par][:], 1.0, GU[par][:, 0:IE], ALU.add, ALU.mult).then_inc(a1, 1)
                dve.wait_ge(a1, n + 1)
                wait_from(dve, h_t, n - 1)
                STT(hb[par][:], th[par][:], scale(row, KAPPA), GU[par][:, IE:2 * IE], ALU.mult,
                    ALU.mult).then_inc(h_rdy, 1)

            def hidden_lo(n, par):
                dve.wait_ge(h_hi, n + 1)
                TT(hx[par][:, IE:2 * IE], HT[:, 0:IE], hx[par][:, 0:IE], ALU.subtract).then_inc(h_lo, 1)

            def accumulate(j):
                dve.wait_ge(gated, j * GATE_STEPS + GATE_STEPS)
                TT(gy[:, 0:1], span(gate, j, 1), scale(SHARED, YINV), ALU.mult).then_inc(gyr, 1)
                dve.wait_ge(dn, unit_no(j) + SU)
                dve.wait_ge(s1_ld, j * 16 + 16)
                dve.wait_ge(gyr, j + 1)
                STT(part(sb1, j), DN[:], gy[:, 0:1], part(sb1, j), ALU.mult, ALU.add).then_inc(dn_free, 1)

            dve.wait_ge(consts, CONSTS)
            stats1(0)
            dve.wait_ge(small_ld, 32)
            link = Link(dve, tables)
            w, u = wu_sb[:, 0:HC], wu_sb[:, HC:2 * HC]
            k_ = [wkvc[:, r, :] for r in range(8)]
            link(nc.vector.tensor_scalar(k_[0], w, 0.0, None, ALU.max))
            link(nc.vector.tensor_scalar(k_[1], k_[0], -1.0, None, ALU.mult))
            link(TT(k_[2], u, k_[1], ALU.max))
            link(TT(k_[3], k_[1], k_[2], ALU.subtract))
            link(TT(k_[4], u, k_[0], ALU.add))
            link(nc.vector.tensor_scalar(k_[5], w, 0.0, None, ALU.min))
            assert link.n == WKVC
            dve.wait_ge(tables_act, 2)
            dve.wait_ge(sq, 1)
            for c in range(HC):
                link(nc.vector.tensor_scalar(growth[:, c * T:(c + 1) * T], decay[:, c * T:(c + 1) * T],
                                             k_[0][:, c:c + 1], k_[3][:, c:c + 1], ALU.mult, ALU.subtract))
            for c in range(HC):
                link(nc.vector.tensor_scalar(decay[:, c * T:(c + 1) * T], decay[:, c * T:(c + 1) * T],
                                             0.0, k_[6][:, c:c + 1], ALU.is_gt, ALU.mult))
            scales(0, ROUTER)
            nc.vector.tensor_scalar(scale(ROUTER, YINV), scale(ROUTER, TANH), 2.0, None,
                                    ALU.mult).then_inc(scale_step, 1)
            dve.wait_ge(w_hi, 1)
            STT(wr_hl[:, 1, :], wr_raw[:], scale(ROUTER, S_GU), wr_hl[:, 0, :], ALU.mult,
                ALU.subtract).then_inc(wr_lo, 1)

            def turn(i, j=None, e=None, shared_split=None):
                is_first, is_last = isinstance(i, int) and i == 0, isinstance(i, int) and i == B - 1
                n = None if j is None else j * SU
                later = n is not None and not (isinstance(j, int) and j == 0)
                keys(i)
                if later:
                    hidden_lo(n - 1, 1)
                if not is_first:
                    residual(i - 1)
                if n is not None:
                    hidden(n, 0, SHARED)
                if later:
                    accumulate(j - 1)
                scans_(i)
                if n is not None:
                    hidden_lo(n, 0)
                    hidden(n + 1, 1, SHARED)
                if not is_first:
                    act_lo(i - 1)
                reciprocals(i, 0)
                if n is not None:
                    hidden_lo(n + 1, 1)
                reciprocals(i, 2)
                if n is not None:
                    hidden(n + 2, 0, SHARED)
                quotient(i)
                if n is not None:
                    hidden_lo(n + 2, 0)
                if not is_last:
                    stats1(i + 1)
                if not is_first:
                    top2_gate(i - 1)
                if e is not None:
                    scales(e + 2, e)
                if shared_split is not None:
                    if shared_split == 0:
                        scales(1, SHARED)
                    shared_lo(shared_split)
                    shared_lo(shared_split + 1)
                if n is not None:
                    hidden(n + 3, 1, SHARED)

            turns(dve, turn)

            def shared_tile(j, last_sum, beside=lambda u: None):
                n = unit_no(j)
                par = n % 2
                hidden_lo(n - 1, 1 - par)
                for u in range(SU):
                    hidden(n + u, (par + u) % 2, SHARED)
                    if u == 0:
                        last_sum()
                    beside(u)
                    if u < SU - 1:
                        hidden_lo(n + u, (par + u) % 2)

            def last_of_mix(u):
                if u == 0:
                    residual(B - 1)
                if u == 1:
                    act_lo(B - 1)
                if u == 2:
                    top2_gate(B - 1)
                    scales(1 + E, E - 1)

            shared_tile(B - LAG, lambda: accumulate(B - LAG - 1), last_of_mix)

            step = Link(dve, rt)

            def te(ap):
                return ap.rearrange("p (t e) -> p t e", t=B)

            def et(ap):
                return ap.rearrange("p (e t) -> p e t", e=E)

            def choice(k, buf):
                return buf[:, :].rearrange("p (t k) -> p t k", k=TOPK)[:, :, k:k + 1]

            def route_choices():
                dve.wait_ge(top, TOP_STEPS * B)
                step(TT(te(r_d), te(lga[:]), choice(0, mxa).to_broadcast([P, B, E]), ALU.subtract))
                step(TT(r_m.rearrange("p (t k) -> p t k", k=TOPK), mxa[:, :].rearrange("p (t k) -> p t k", k=TOPK),
                        choice(0, mxa).to_broadcast([P, B, TOPK]), ALU.subtract))
                assert step.n == RT_EXP
                for k, one in enumerate((r_one0, r_one1)):
                    step(TT(te(one), iota8[:].unsqueeze(1).to_broadcast([P, B, E]),
                            choice(k, ixa).to_broadcast([P, B, E]), ALU.is_equal))
                step(TT(r_mask, r_one0, r_one1, ALU.add))
                assert step.n == RT_MASK
                dve.wait_ge(rt_exp, 2)
                step(nc.vector.tensor_reduce(r_sum, te(r_d), AX.X, ALU.add))
                step(nc.vector.reciprocal(r_inv, r_sum))
                for k in range(TOPK):
                    step(TT(w12[:, k, :].unsqueeze(2), choice(k, r_m), r_inv.unsqueeze(2), ALU.mult))

            def route_slots():
                dve.wait_ge(rt_sums, 1)
                step(nc.vector.tensor_copy(et(r_tot), LG[:, 0:B * E].rearrange("p (t e) -> p e t", t=B)))
                step(nc.vector.tensor_tensor_scan(r_incl, restart[:], r_tot, 0.0, ALU.mult, ALU.add))
                step(TT(r_tot, r_incl, r_tot, ALU.subtract))
                count = et(r_incl)[:, :, B - 1:B]
                step(nc.vector.tensor_scalar(r_cnt.unsqueeze(2), count, float(P - 1), None, ALU.add))
                step(nc.vector.tensor_scalar(r_cnt, r_cnt, P.bit_length() - 1, None, ALU.logical_shift_right))
                step(nc.vector.tensor_copy(r_tiles, r_cnt))
                step(nc.vector.tensor_tensor_scan(r_end, ones[:, 0:E], r_tiles, 0.0, ALU.mult, ALU.add))
                step(TT(r_off, r_end, r_tiles, ALU.subtract))
                step(STT(et(r_tot), r_off.unsqueeze(2).to_broadcast([P, E, B]), float(P), et(r_tot),
                         ALU.mult, ALU.add))
                step(TT(te(r_pos), KT[:, 0:B * E].rearrange("p (t e) -> p t e", t=B),
                        r_tot.rearrange("p (e t) -> p t e", e=E), ALU.add))
                for k, one in enumerate((r_one0, r_one1)):
                    step(TT(r_prod, r_pos, one, ALU.mult))
                    step(nc.vector.tensor_reduce(r_posf[:, k * B:(k + 1) * B], te(r_prod), AX.X, ALU.add))
                nc.vector.tensor_copy(posi[:, :, :].rearrange("p k t -> p (k t)"), r_posf).then_inc(rt_pos, 1)
                step(TT(r_cmp.rearrange("p (j e) -> p j e", e=E), iotaj[:].unsqueeze(2).to_broadcast([P, NSLOT, E]),
                        r_end.unsqueeze(1).to_broadcast([P, NSLOT, E]), ALU.is_ge))
                step(nc.vector.tensor_reduce(r_eid, r_cmp.rearrange("p (j e) -> p j e", e=E), AX.X, ALU.add))
                nc.vector.tensor_scalar(eidi[:], r_eid, float(E - 1), None, ALU.min).then_inc(rt_pos, 1)

            route_choices()
            for j in range(B - LAG + 1, SH1):
                if j == B - LAG + 1:
                    shared_tile(j, lambda: accumulate(j - 1), lambda u: route_slots() if u == 0 else None)
                else:
                    shared_tile(j, lambda: accumulate(j - 1))

            dve.wait_ge(ids_ld, 16)
            nc.vector.tensor_copy(ids_float, ids_back).then_inc(ids_f, 1)
            dve.wait_ge(ids_t, 1)
            nc.vector.tensor_copy(idsi[:], KT[:, 0:NSLOT]).then_inc(ids_rdy, 1)

            def gathered_lo(j, r):
                dve.wait_ge(g_hi, j + 1)
                STT(xe[r][:, H:2 * H], XT[:], XS, xe[r][:, 0:H], ALU.mult, ALU.subtract).then_inc(g_lo, 1)

            def expert_rows(j, r, e):
                dve.wait_ge(dn, N_EXP + j + 1)
                if isinstance(j, int) and j < 2:
                    dve.wait_ge(acc_st, 16 * SH1)
                else:
                    dve.wait_ge(y_st, j * 16 - 16)
                nc.vector.tensor_scalar(sb1[:, r * H:(r + 1) * H], DN[:], scale(e, YINV), None,
                                        ALU.mult).then_inc(dn_free, 1)

            def expert_unit(j, r, before, ahead=True):
                e = dve.value_load(span(eidi[0:1, :], j, 1), min_val=0, max_val=E - 1)
                hidden_lo(N_EXP + j - 1, (N_EXP + 1 + r) % 2)
                if ahead:
                    gathered_lo(j + 1, 1 - r)
                hidden(N_EXP + j, (N_EXP + r) % 2, e)
                if before is None:
                    accumulate(SH1 - 1)
                else:
                    ep = dve.value_load(span(eidi[0:1, :], j - 1, 1), min_val=0, max_val=E - 1)
                    expert_rows(j - 1, 1 - r, ep)
                return e

            dve.wait_ge(rt_pos, 2)
            gathered_lo(0, 0)
            expert_unit(0, 0, None)
            expert_unit(1, 1, True)
            expert_unit(2, 0, True)
            with dve.Fori(1, (NSLOT - 3) // 2) as m:
                expert_unit(m * 2 + 1, 1, True)
                expert_unit(m * 2 + 2, 0, True)
            expert_unit(NSLOT - 2, 1, True)
            last_e = expert_unit(NSLOT - 1, 0, True, ahead=False)

            def combine(t):
                dve.wait_ge(acc_ld[t % 2], 16 * (t // 2 + 1))
                dve.wait_ge(cgather[t % 2], 32 * (t // 2 + 1))
                for k, done in enumerate((comb1, comb2)):
                    STT(combine_row(t, 0), combine_row(t, 1 + k), w12[:, k, t:t + 1], combine_row(t, 0),
                        ALU.mult, ALU.add).then_inc(done, 1)
                    if k == 0:
                        dve.wait_ge(comb1, t + 1)

            def combines(first, last):
                def beside(u):
                    for t in range(first, last):
                        if (t - first) * SU // (last - first) == u:
                            combine(t)
                return beside

            shared_tile(SH1, lambda: expert_rows(NSLOT - 1, 0, last_e))
            shared_tile(SH1 + 1, lambda: accumulate(SH1), combines(0, COMB1))
            shared_tile(SH1 + 2, lambda: accumulate(SH1 + 1), combines(COMB1, COMB2))
            n = unit_no(B - 1) + SU - 1
            hidden_lo(n, n % 2)
            accumulate(B - 1)
            for t in range(COMB2, B):
                combine(t)


def kernel(**inputs):
    import numpy as np
    from concourse import bacc
    from concourse.bass_utils import run_bass_kernel_spmd

    def halves(gate, up):
        both = np.stack([gate.reshape(-1, IE, HC, P), up.reshape(-1, IE, HC, P)], axis=1)
        return both.transpose(0, 4, 3, 1, 2).reshape(-1, P, GUW)

    def downs(w):
        return w.reshape(-1, H, IC, P).transpose(0, 3, 2, 1).reshape(-1, P, DW)

    a = {n: np.asarray(v) for n, v in inputs.items()}
    ffn = {n[len("L0_ffn_"):]: v for n, v in a.items() if n.startswith("L0_ffn_")}
    wr = np.concatenate([ffn["gate_w"], ffn["shared_expert_gate_w"]], axis=0)
    arrays = {
        "x": a["x"].reshape(B * T, H),
        "ctx_t": a["ctx_2048"].reshape(B, T, HC, P).transpose(0, 3, 2, 1).reshape(B * P, HC * T),
        "wu": np.concatenate([a["L0_xattn_w"].reshape(HC, P).T, a["L0_xattn_u"].reshape(HC, P).T], axis=1),
        "wr": wr.reshape(RN, HC, P).transpose(2, 1, 0).reshape(P, HC * RN),
        "wgu": np.concatenate([halves(ffn["expert_gate_w"], ffn["expert_up_w"]),
                               halves(ffn["shared_gate_w"], ffn["shared_up_w"])], axis=0),
        "wd": np.concatenate([downs(ffn["expert_down_w"]),
                              downs(ffn["shared_down_w"].reshape(H, SU, IE).transpose(1, 0, 2))], axis=0),
    }
    arrays = {n: np.ascontiguousarray(v) for n, v in arrays.items()}
    nc = bacc.Bacc("TRN2", target_bir_lowering=False, num_devices=1)
    aps = {n: nc.dram_tensor(n, v.shape, F32, kind="ExternalInput").ap() for n, v in arrays.items()}
    out = nc.dram_tensor("out", (B * T, H), F32, kind="ExternalOutput").ap()
    build(nc, **aps, out=out)
    r = run_bass_kernel_spmd(nc, [arrays], core_ids=[0])
    return r.results[0]["out"].reshape(B, T, H)
```

```python
from contextlib import ExitStack

import concourse.bass as bass
from concourse import mybir

F32, F16, I32, U32 = mybir.dt.float32, mybir.dt.float16, mybir.dt.int32, mybir.dt.uint32
ALU, ACT, AX = mybir.AluOpType, mybir.ActivationFunctionType, mybir.AxisListType
ds = bass.ds

P = 128
B, T, H = 16, 128, 512
E, IE, IS, TOPK = 8, 256, 1024, 2
HC = H // P
IC = IE // P
SU = IS // IE
NSLOT = (TOPK * B * T + E * (P - 1)) // P
GUW, DW = HC * 2 * IE, IC * H
UW = GUW + DW
LAG = 3
NX = LAG + 1
NB = 6
SPLIT0 = 1
XS = 1024.0
EPS = 1e-5
RN = E + 1
SHARED, ROUTER = E, E + 1
S_GU, S_D, TANH, KAPPA, YINV = range(5)
HI_LO = [(0, 0), (0, 1), (1, 0)]
WKV0 = E * UW
SH0 = WKV0 + 4 * 2 * H
N_EXP = SU * B
GATHERS = 4
PADS = B * T
TOP_STEPS, GATE_STEPS, NORM_STEPS, SCALE_STEPS = 5, 1, 4, 10
CONSTS, WKVC = 17, 6
RT_EXP, RT_MASK = 2, 5


def wait_from(eng, sem, value):
    if not (isinstance(value, int) and value <= 0):
        eng.wait_ge(sem, value)


def span(ap, start, n):
    return ap[:, start:start + n] if isinstance(start, int) else ap[:, ds(start, n)]


def rows(dram, t):
    return dram[t * P:(t + 1) * P, :] if isinstance(t, int) else dram[ds(t * P, P), :]


def turns(eng, turn):
    for i in range(SPLIT0):
        turn(i)
    turn(SPLIT0, shared_split=0)
    turn(SPLIT0 + 1, shared_split=2)
    turn(LAG, j=0, se=0)
    turn(LAG + 1, j=1, se=1, he=0)
    with eng.Fori(LAG + 2, LAG + E - 1) as i:
        turn(i, j=i - LAG, se=i - LAG, he=i - (LAG + 1), le=i - (LAG + 2))
    turn(LAG + E - 1, j=E - 1, he=E - 2, le=E - 3)
    turn(LAG + E, j=E, le=E - 2)
    with eng.Fori(LAG + E + 1, B - 2) as i:
        turn(i, j=i - LAG)
    turn(B - 2, j=B - 2 - LAG)
    turn(B - 1, j=B - 1 - LAG)


class Link:

    def __init__(self, eng, sem):
        self.eng, self.sem, self.n = eng, sem, 0

    def __call__(self, ins):
        self.n += 1
        ins.then_inc(self.sem, 1)
        self.eng.wait_ge(self.sem, self.n)


def build(nc, x, ctx_t, wu, wr, wgu, wd, out):
    ctx = ExitStack()
    with ctx:
        def sb(name, shape, dt=F32):
            return ctx.enter_context(nc.sbuf_tensor(name, shape, dt))

        def bank(name):
            return ctx.enter_context(nc.psum_tensor(name, [P, 512], F32))

        def sems(names):
            return [ctx.enter_context(nc.semaphore(n)) for n in names.split()]

        xn_dram = nc.dram_tensor("xn_rows", (B * T + P, H), F32).ap()
        ids_dram = nc.dram_tensor("slots", (NSLOT * P, 2), I32).ap()

        wall = sb("wall", [P, SH0 + SU * UW])
        wall16 = wall[:, :].bitcast(F16)
        xt = sb("xt", [P, NX * 2 * H], F16)
        xb, cb = sb("xb", [P, NB * H]), sb("cb", [P, 2 * H])
        kb, yb, xnb = sb("kb", [P, H]), sb("yb", [P, H]), sb("xnb", [P, H])
        growth, decay = sb("growth", [P, HC * T]), sb("decay", [P, HC * T])
        th = [sb(f"th{i}", [P, IE]) for i in range(2)]
        hb = [sb(f"hb{i}", [P, IE]) for i in range(2)]
        hx = [sb(f"hx{i}", [P, 2 * IE], F16) for i in range(2)]
        junk = sb("junk", [P, GUW // 2], mybir.dt.bfloat16)
        ident, ones, tri = sb("ident", [P, P]), sb("ones", [P, P]), sb("tri", [P, P])
        wkvc, wu_sb = sb("wkvc", [P, 8, HC]), sb("wu_sb", [P, 2 * HC])
        wr_raw, wr_hl = sb("wr_raw", [P, HC * RN]), sb("wr_hl", [P, 2, HC * RN], F16)
        st6, mv, nrm = sb("st6", [P, 2, 6]), sb("mv", [P, 2, 2]), sb("nrm", [P, 2, 4])
        mhalf, warm = sb("mhalf", [P, 1]), sb("warm", [P, 1])
        ssq, ssqe = sb("ssq", [P, 2 * SU]), sb("ssqe", [P, 4])
        scw, scf, sci = sb("scw", [P, 2]), sb("scf", [P, 10]), sb("sci", [P, 9], I32)
        scl = sb("scl", [P, (E + 2) * 5])
        lgt, mx8, ix8 = sb("lgt", [P, RN]), sb("mx8", [P, 8]), sb("ix8", [P, 8], U32)
        sg = sb("sg", [P, 1])
        lga, mxa, ixa = sb("lga", [P, B * E]), sb("mxa", [P, B * TOPK]), sb("ixa", [P, B * TOPK])
        gate = sb("gate", [P, B])
        posi, pairs = sb("posi", [P, TOPK, B], I32), sb("pairs", [P, TOPK, B, 2], I32)
        eidi, idsi, wsl = sb("eidi", [P, NSLOT], I32), sb("idsi", [P, NSLOT], I32), sb("wsl", [P, NSLOT])
        idx = [sb(f"idx{i}", [P, 1], I32) for i in range(GATHERS)]
        adx = [sb(f"adx{i}", [P, 1], I32) for i in range(2)]

        iota8, iotaj, restart = sb("iota8", [P, E]), sb("iotaj", [P, NSLOT]), sb("restart", [P, E * B])
        gy = sb("gy", [P, 2])

        def taken(n, at=[0]):
            at[0] += n
            return cb[:, at[0] - n:at[0]]

        r_d, r_m, r_one0, r_one1, r_mask = taken(B * E), taken(B * TOPK), taken(B * E), taken(B * E), taken(B * E)
        r_tot, r_incl, r_pos, r_prod = growth[:, 0:128], growth[:, 128:256], growth[:, 256:384], growth[:, 384:512]
        r_sum, r_inv, r_posf = taken(B), taken(B), taken(TOPK * B)
        r_cnt, r_tiles, r_end, r_off = taken(E).bitcast(I32), taken(E), taken(E), taken(E)
        r_cmp, r_eid = taken(NSLOT * E), taken(NSLOT)
        ids_back = yb[0:NSLOT, 0:2 * P].bitcast(I32).rearrange("j (p a) -> j p a", a=2)
        ids_float, ids_weight = yb[0:NSLOT, 2 * P:3 * P], yb[0:NSLOT, 3 * P:4 * P]

        late = [(B - NB + k) % NB for k in range(NB)]
        xg = [xb[:, k * H:(k + 1) * H] for k in late[0:GATHERS]]
        ye = [xb[:, k * H:(k + 1) * H] for k in late[GATHERS:]]
        xe = [kb[:, :].bitcast(F16), xnb[:, :].bitcast(F16)]

        KT, YT, XT, LG = bank("KT"), bank("YT"), bank("XT"), bank("LG")
        GU = [bank("GU0"), bank("GU1")]
        HT, DN = bank("HT"), bank("DN")

        small_ld, x_ld, c_ld, e_ld = sems("small_ld x_ld c_ld e_ld")
        sh_ld = sems("sh_ld0 sh_ld1 sh_ld2 sh_ld3")
        xn_st, out_st, added = sems("xn_st out_st added")
        consts, tables, tables_act = sems("consts tables tables_act")
        stat1, agg1, norm1, k_rdy, k_t, kp1, exps, v1, v2 = sems(
            "stat1 agg1 norm1 k_rdy k_t kp1 exps v1 v2")
        scans, nd, rcp, ymul, y_rdy, y_t, x1_rdy, stat2, agg2, norm2 = sems(
            "scans nd rcp ymul y_rdy y_t x1_rdy stat2 agg2 norm2")
        xn_rdy, xn_t, x_hi, x_lo, logits, lg_rdy, gate_tanh, top, gated = sems(
            "xn_rdy xn_t x_hi x_lo logits lg_rdy gate_tanh top gated")
        gu, tanh, a1, h_rdy, h_t, h_hi, h_lo, dn, dn_free = sems("gu tanh a1 h_rdy h_t h_hi h_lo dn dn_free")
        sq, sq_sum, sq_red, exponents, scale_step, w_hi, w_ws, w_lo = sems(
            "sq sq_sum sq_red exponents scale_step w_hi w_ws w_lo")
        rt, rt_exp, rt_sums, rt_pos, ids_zero, ids_zst, scattered, ids_ld, ids_f, ids_t, ids_rdy = sems(
            "rt rt_exp rt_sums rt_pos ids_zero ids_zst scattered ids_ld ids_f ids_t ids_rdy")
        gather = sems("gather0 gather1 gather2 gather3")
        idx_rdy, adx_rdy, g_t, g_hi, g_lo, wr_lo, gyr, waited = sems(
            "idx_rdy adx_rdy g_t g_hi g_lo wr_lo gyr waited")

        def wkv(t, r, n=1):
            if isinstance(t, int):
                return wall[:, WKV0 + ((t % 2) * 4 + r) * H:WKV0 + ((t % 2) * 4 + r + n) * H]
            return wall[:, ds((t % 2) * (4 * H) + (WKV0 + r * H), n * H)]

        def wkv_chunk(t, r, c):
            off = WKV0 + r * H + c * T
            if isinstance(t, int):
                return wall[:, (t % 2) * 4 * H + off:(t % 2) * 4 * H + off + T]
            return wall[:, ds((t % 2) * (4 * H) + off, T)]

        def part(buf, t):
            return buf[:, (t % 2) * H:(t % 2 + 1) * H] if isinstance(t, int) else buf[:, ds((t % 2) * H, H)]

        def xrow(t):
            return span(xb, (t % NB) * H, H)

        def xt_row(t, lo):
            return span(xt, (t % NX) * (2 * H) + lo * H, H)

        def split(base, off, n):
            return wall16[:, 2 * base + off:2 * base + off + n] if isinstance(base, int) \
                else wall16[:, ds(base * 2 + off, n)]

        def gate_up(base, lo, c, n=1):
            return split(base, lo * GUW + c * 2 * IE, n * 2 * IE)

        def down(base, lo, c, n=1):
            return split(base, 2 * GUW + lo * DW + c * H, n * H)

        def scale(row, k):
            return span(scl, row * 5 + k, 1)

        def sh_base(s):
            return SH0 + s * UW

        def plain(eng):
            eng.sem_inc(waited, 1)

        block = ctx.enter_context(nc.Block())

        @block.sync
        def _(sp):
            def load_x(t):
                wait_from(sp, out_st, (t - (NB - 1)) * 16)
                plain(sp)
                wait_from(sp, x_ld, t * 16)
                plain(sp)
                sp.dma_start(xrow(t), rows(x, t)).then_inc(x_ld, 16)

            def load_ctx(t):
                wait_from(sp, y_rdy, t - 1)
                plain(sp)
                wait_from(sp, c_ld, t * 16)
                plain(sp)
                sp.dma_start(part(cb, t), rows(ctx_t, t)).then_inc(c_ld, 16)

            def store_xn(t):
                sp.wait_ge(xn_rdy, t + 1)
                plain(sp)
                sp.dma_start(rows(xn_dram, t), xnb[:]).then_inc(xn_st, 16)

            def store_sum(j):
                sp.wait_ge(dn_free, j + 1)
                plain(sp)
                wait_from(sp, out_st, j * 16)
                plain(sp)
                sp.dma_start(rows(out, j), xrow(j)).then_inc(out_st, 16)

            def load_expert(e):
                base = (e + 1) * UW
                wait_from(sp, e_ld, e * 32)
                plain(sp)
                sp.wait_ge(w_lo, SU)
                src = (wgu[e], wd[e]) if isinstance(e, int) else tuple(
                    w[ds(e, 1), :, :].rearrange("a p n -> (a p) n") for w in (wgu, wd))
                sp.dma_start(span(wall, base, GUW), src[0]).then_inc(e_ld, 16)
                sp.dma_start(span(wall, base + GUW, DW), src[1]).then_inc(e_ld, 16)

            sp.dma_start(wu_sb[:], wu).then_inc(small_ld, 16)
            sp.dma_start(wr_raw[:], wr).then_inc(small_ld, 16)
            load_x(0)
            load_ctx(0)
            for s in range(SU):
                sp.dma_start(span(wall, (4 + s) * UW, GUW), wgu[E + s]).then_inc(sh_ld[s], 16)
                sp.dma_start(span(wall, (4 + s) * UW + GUW, DW), wd[E + s]).then_inc(sh_ld[s], 16)
                if s == 0:
                    load_x(1)
                    load_ctx(1)
            sp.wait_ge(ids_zero, 3)
            sp.dma_start(ids_dram.rearrange("(j p) a -> j (p a)", p=P),
                         xnb[0:NSLOT, 0:2 * P].bitcast(I32)).then_inc(ids_zst, 16)
            sp.dma_start(xn_dram[PADS:PADS + P, :], yb[:]).then_inc(ids_zst, 16)
            sp.dma_start(out[PADS:PADS + P, :], yb[:]).then_inc(ids_zst, 16)

            def turn(i, j=None, se=None, he=None, le=None, shared_split=None):
                is_first, is_last = isinstance(i, int) and i == 0, isinstance(i, int) and i == B - 1
                if not is_first and not is_last:
                    load_ctx(i + 1)
                if se is not None:
                    load_expert(se)
                if not is_first:
                    store_xn(i - 1)
                if j is not None and not (isinstance(j, int) and j == 0):
                    store_sum(j - 1)
                if not (isinstance(i, int) and i >= B - 2):
                    load_x(i + 2)

            turns(sp, turn)
            store_xn(B - 1)
            sp.wait_ge(y_rdy, B)
            load_expert(E - 1)
            for j in range(B - LAG - 1, B - 1):
                store_sum(j)
            sp.wait_ge(scattered, TOPK * B * 16)
            sp.dma_start(ids_back.rearrange("j p a -> j (p a)"),
                         ids_dram.rearrange("(j p) a -> j (p a)", p=P)).then_inc(ids_ld, 16)
            store_sum(B - 1)
            sp.wait_ge(out_st, 16 * B)
            sp.wait_ge(added, 16 * NSLOT)

        @block.gpsimd
        def _(pool):
            link = Link(pool, consts)
            pool.memset(yb[:], 0.0).then_inc(ids_zero, 1)
            slots = xnb[0:NSLOT, 0:2 * P].bitcast(I32).rearrange("j (p a) -> j p a", a=2)
            pool.memset(slots[:, :, 1:2], 0).then_inc(ids_zero, 1)
            pool.iota(slots[:, :, 0:1], [[1, P]], base=PADS, channel_multiplier=0).then_inc(ids_zero, 1)
            for buf in (ssq, ssqe, scf, sci):
                link(pool.memset(buf[:], 0))
            link(pool.memset(mhalf[:], -0.5))
            link(pool.memset(ones[:], 1.0))
            link(pool.memset(ident[:], 0.0))
            link(pool.affine_select(out=ident[:], in_=ident[:], compare_op=ALU.not_equal, fill=1.0,
                                    base=0, pattern=[[-1, P]], channel_multiplier=1))
            link(pool.affine_select(out=tri[:], in_=ones[:], compare_op=ALU.is_gt, fill=0.0,
                                    base=0, pattern=[[1, P]], channel_multiplier=-1))
            link(pool.iota(decay[:], [[0, HC], [1, T]], base=0, channel_multiplier=0,
                           allow_small_or_imprecise_dtypes=True))
            for k in range(TOPK):
                link(pool.iota(pairs[:, k, :, 0:1], [[P, B]], base=0, channel_multiplier=1))
            for buf, pattern in (iota8, [[1, E]]), (iotaj, [[1, NSLOT]]), (restart, [[0, E], [1, B]]):
                link(pool.iota(buf[:], pattern, base=0, channel_multiplier=0,
                               allow_small_or_imprecise_dtypes=True))
            link(pool.tensor_scalar(restart[:], restart[:], 1.0, None, ALU.min))
            link(pool.memset(warm[:], 0.0))
            assert link.n == CONSTS

            def norm(t, k, stats_rdy, steps, used):
                pool.wait_ge(stats_rdy, t + 1)
                wait_from(pool, used, t)
                plain(pool)
                nc.gpsimd.tensor_scalar(nrm[:, k, 0:1], mv[:, k, 1:2], EPS, None, ALU.add).then_inc(steps, 1)
                nc.gpsimd.tensor_scalar(nrm[:, k, 1:2], mv[:, k, 0:1], -1.0, None, ALU.mult).then_inc(steps, 1)
                pool.wait_ge(steps, t * NORM_STEPS + 2)
                nc.gpsimd.tensor_tensor(nrm[:, k, 2:3], nrm[:, k, 0:1], mhalf[:], ALU.pow).then_inc(steps, 1)
                pool.wait_ge(steps, t * NORM_STEPS + 3)
                nc.gpsimd.tensor_tensor(nrm[:, k, 3:4], nrm[:, k, 1:2], nrm[:, k, 2:3], ALU.mult).then_inc(steps, 1)

            def second_product(t):
                pool.wait_ge(c_ld, t * 16 + 16)
                pool.wait_ge(exps, t + 1)
                nc.gpsimd.tensor_tensor(wkv(t, 3), wkv(t, 2), part(cb, t), ALU.mult).then_inc(v2, 1)

            def expert_lo(e, k):
                raw = (e + 1) * UW + k * (GUW // 2)
                hi, lo = (gate_up(e * UW, q, 0, HC) if k < 2 else down(e * UW, q, 0, IC) for q in range(2))
                if k == 0:
                    pool.wait_ge(w_ws, e * 3 + 3)
                if k < 2:
                    half = GUW // 2
                    hi, lo = split(e * UW, k * half, half), split(e * UW, GUW + k * half, half)
                ins = nc.gpsimd.tensor_tensor(lo, span(wall, raw, GUW // 2), hi, ALU.subtract)
                if k == 2:
                    ins.then_inc(w_lo, 1)

            def scales(k, row):
                base = 0 if isinstance(k, int) and k == 0 else k * SCALE_STEPS + 1
                TS, n = nc.gpsimd.tensor_scalar, 0

                def step(ins, wait=True):
                    nonlocal n
                    n += 1
                    ins.then_inc(scale_step, 1)
                    if wait:
                        pool.wait_ge(scale_step, base + n)
                        plain(pool)

                pool.wait_ge(exponents, k * 3 + 3)
                plain(pool)
                field = [scf[:, 4 + f:5 + f] for f in range(5)]
                e_gu, e_d, h_gu, h_d, tmp = (scf[:, c:c + 1] for c in (0, 1, 2, 3, 9))
                step(TS(scf[:, 0:4], sci[:, 0:4], 1.0, None, ALU.mult))
                step(TS(scf[:, 4:6], scf[:, 2:4], -1.0, 205.0, ALU.mult, ALU.add), False)
                step(TS(field[TANH], h_gu, 38.0, None, ALU.add), False)
                step(TS(tmp, h_gu, 2.0, 83.0, ALU.mult, ALU.add), False)
                step(TS(field[YINV], e_gu, -84.0, None, ALU.add))
                step(nc.gpsimd.tensor_tensor(field[KAPPA], tmp, e_gu, ALU.subtract), False)
                step(nc.gpsimd.tensor_tensor(field[YINV], field[YINV], h_d, ALU.add))
                step(TS(field[YINV], field[YINV], 0.0, 254.0, ALU.max, ALU.min))
                step(TS(sci[:, 4:9], scf[:, 4:9], float(1 << 23), None, ALU.mult))
                step(pool.tensor_copy(span(scl, row * 5, 5).bitcast(I32), sci[:, 4:9]))
                assert n == SCALE_STEPS

            norm(0, 0, agg1, norm1, k_rdy)
            scales(0, ROUTER)
            nc.gpsimd.tensor_scalar(scale(ROUTER, YINV), scale(ROUTER, TANH), 2.0, None,
                                    ALU.mult).then_inc(scale_step, 1)

            def turn(i, j=None, se=None, he=None, le=None, shared_split=None):
                if le is not None:
                    expert_lo(le, 0)
                if not (isinstance(i, int) and i == 0):
                    norm(i - 1, 1, agg2, norm2, xn_rdy)
                if not (isinstance(i, int) and i == B - 1):
                    norm(i + 1, 0, agg1, norm1, k_rdy)
                second_product(i)
                if le is not None:
                    expert_lo(le, 1)
                    expert_lo(le, 2)
                if se is not None:
                    scales(se + 2, se)
                if shared_split == 0:
                    scales(1, SHARED)

            turns(pool, turn)
            norm(B - 1, 1, agg2, norm2, xn_rdy)
            scales(E + 1, E - 1)

            pool.wait_ge(ids_zst, 48)
            pool.wait_ge(rt_pos, 1)
            for t in range(B):
                for k in range(TOPK):
                    pool.indirect_dma_start(ids_dram, bass.IndirectOffsetOnAxis(ap=posi[:, k, t:t + 1], axis=0),
                                            pairs[:, k, t, :], None).then_inc(scattered, 16)
            for k in range(3):
                expert_lo(E - 1, k)

            pool.wait_ge(ids_rdy, 2)
            pool.wait_ge(xn_st, 16 * B)
            pool.wait_ge(out_st, 16 * (B - 2))

            def gather_tile(j, r):
                if not isinstance(j, int):
                    pool.wait_ge(gather[r], (j - r) // GATHERS * 16)
                elif j >= GATHERS:
                    pool.wait_ge(gather[r], j // GATHERS * 16)
                pool.tensor_copy(idx[r][:], span(idsi, j, 1)).then_inc(idx_rdy, 1)
                wait_from(pool, g_t, j - GATHERS + 1)
                plain(pool)
                pool.wait_ge(idx_rdy, j + 1)
                plain(pool)
                pool.indirect_dma_start(xg[r], None, xn_dram, bass.IndirectOffsetOnAxis(ap=idx[r][:, 0:1], axis=0)
                                        ).then_inc(gather[r], 16)

            def add_rows(j, r):
                wait_from(pool, added, j * 16)
                plain(pool)
                pool.tensor_copy(adx[r][:], span(idsi, j, 1)).then_inc(adx_rdy, 1)
                pool.wait_ge(dn_free, j + (B + 1))
                plain(pool)
                pool.wait_ge(adx_rdy, j + 1)
                plain(pool)
                pool.indirect_dma_start(out, bass.IndirectOffsetOnAxis(ap=adx[r][:, 0:1], axis=0), ye[r], None,
                                        compute_op=ALU.add).then_inc(added, 16)

            for j in range(GATHERS + 1):
                gather_tile(j, j % GATHERS)
            pool.wait_ge(out_st, 16 * B)
            for j in range(GATHERS + 1, 2 * GATHERS):
                gather_tile(j, j % GATHERS)
                add_rows(j - (GATHERS + 1), (j + 1) % 2)
            with pool.Fori(2, (NSLOT - GATHERS) // GATHERS + 1) as m:
                for r in range(GATHERS):
                    gather_tile(m * GATHERS + r, r)
                    add_rows(m * GATHERS + (r - (GATHERS + 1)), (r + 1) % 2)
            for j in range(NSLOT // GATHERS * GATHERS, NSLOT):
                gather_tile(j, j % GATHERS)
                add_rows(j - (GATHERS + 1), (j + 1) % 2)
            for j in range(NSLOT - (GATHERS + 1), NSLOT):
                add_rows(j, j % 2)

        @block.scalar
        def _(act):
            def square(src, junk, n, out1):
                nc.scalar.activation(junk, src, ACT.Square, accum_out=out1).then_inc(sq, 1)

            act.wait_ge(consts, CONSTS)
            nc.scalar.activation(warm[:], mhalf[:], ACT.Tanh).then_inc(tables_act, 1)
            act.wait_ge(tables, WKVC)
            nc.scalar.activation(wkvc[:, 6, :], wkvc[:, 5, :], ACT.Exp).then_inc(tables_act, 1)
            act.wait_ge(small_ld, 32)
            square(wr_raw[:], junk[:, 0:HC * RN], HC * RN, ssqe[:, 0:1])

            def first_norm(t):
                act.wait_ge(norm1, (t + 1) * NORM_STEPS)
                wait_from(act, k_t, t)
                plain(act)
                nc.scalar.activation(kb[:], xrow(t), ACT.Identity, bias=nrm[:, 0, 3:4],
                                     scale=nrm[:, 0, 2:3]).then_inc(k_rdy, 1)

            def second_norm(t):
                act.wait_ge(norm2, (t + 1) * NORM_STEPS)
                wait_from(act, xn_t, t)
                wait_from(act, xn_st, 16 * t)
                if isinstance(t, int) and t == 0:
                    act.wait_ge(ids_zst, 48)
                plain(act)
                nc.scalar.activation(xnb[:], xrow(t), ACT.Identity, bias=nrm[:, 1, 3:4],
                                     scale=nrm[:, 1, 2:3]).then_inc(xn_rdy, 1)

            def both_exps(t):
                act.wait_ge(kp1, t + 1)
                wait_from(act, ymul, t - 1)
                plain(act)
                for c in range(HC):
                    nc.scalar.activation(wkv_chunk(t, 2, c), wkv_chunk(t, 1, c), ACT.Exp, bias=wkvc[:, 4, c:c + 1])
                nc.scalar.activation(wkv(t, 0), wkv(t, 1), ACT.Exp).then_inc(exps, 1)

            def act_hi(t):
                act.wait_ge(xn_t, t + 1)
                if not isinstance(t, int) or t >= NX:
                    act.wait_ge(gu, (t - NX + 1) * SU)
                plain(act)
                nc.scalar.activation(xt_row(t, 0), XT[:], ACT.Copy, scale=XS).then_inc(x_hi, 1)

            def router_out(t):
                act.wait_ge(logits, t + 1)
                wait_from(act, top, t * TOP_STEPS)
                nc.scalar.activation(lgt[:], LG[:, 0:RN], ACT.Copy, scale=scale(ROUTER, YINV)).then_inc(lg_rdy, 1)
                act.wait_ge(lg_rdy, t + 1)
                wait_from(act, gated, t * GATE_STEPS)
                nc.scalar.activation(sg[:], lgt[:, E:E + 1], ACT.Tanh, scale=0.5).then_inc(gate_tanh, 1)

            def unit_tanh(n, par, row):
                act.wait_ge(gu, n + 1)
                wait_from(act, h_rdy, n - 1)
                plain(act)
                nc.scalar.activation(th[par][:], GU[par][:, 0:IE], ACT.Tanh, scale=scale(row, TANH)).then_inc(tanh, 1)

            def unit_hi(n, par):
                act.wait_ge(h_t, n + 1)
                wait_from(act, dn, n - 1)
                nc.scalar.activation(hx[par][:, 0:IE], HT[:, 0:IE], ACT.Copy).then_inc(h_hi, 1)

            def shared_square(s):
                act.wait_ge(sh_ld[s], 32)
                wait_from(act, sq_sum, 1)
                raw = (4 + s) * UW
                square(span(wall, raw, GUW), span(wall, s * UW, GUW), GUW, ssq[:, s:s + 1])
                square(span(wall, raw + GUW, DW), span(wall, s * UW + GUW, DW), DW, ssq[:, SU + s:SU + s + 1])

            def shared_hi(s):
                raw = (4 + s) * UW
                act.wait_ge(scale_step, 2 * SCALE_STEPS + 1)
                nc.scalar.activation(gate_up(sh_base(s), 0, 0, HC), span(wall, raw, GUW), ACT.Copy,
                                     scale=scale(SHARED, S_GU)).then_inc(w_hi, 1)
                nc.scalar.activation(down(sh_base(s), 0, 0, IC), span(wall, raw + GUW, DW), ACT.Copy,
                                     scale=scale(SHARED, S_D)).then_inc(w_hi, 1)

            def expert_square(e, k):
                if k == 0:
                    act.wait_ge(e_ld, (e + 1) * 32)
                    plain(act)
                    act.wait_ge(sq_sum, e + 2)
                act.wait_ge(sq, e * 3 + (2 * SU + 1 + k))
                plain(act)
                n = GUW // 2
                square(span(wall, (e + 1) * UW + k * n, n), junk[:], n, ssqe[:, (0, 2, 1)[k]:(0, 2, 1)[k] + 1])

            def expert_piece(e, k):
                half = GUW // 2
                raw = span(wall, (e + 1) * UW + k % 3 * half, half)
                if k == 0:
                    act.wait_ge(scale_step, e * SCALE_STEPS + (3 * SCALE_STEPS + 1))
                    plain(act)
                    act.wait_ge(w_lo, e + SU)
                    plain(act)
                if k < 3:
                    hi = split(e * UW, k * half, half) if k < 2 else down(e * UW, 0, 0, IC)
                    nc.scalar.activation(hi, raw, ACT.Copy, scale=scale(e, S_GU if k < 2 else S_D)).then_inc(w_hi, 1)
                else:
                    act.wait_ge(w_hi, e * 3 + (2 * SU + 2 + k - 3))
                    plain(act)
                    nc.scalar.activation(raw, raw, ACT.Copy, scale=scale(e, S_GU if k < 5 else S_D)).then_inc(w_ws, 1)

            first_norm(0)
            act.wait_ge(scale_step, SCALE_STEPS + 1)
            nc.scalar.activation(wr_hl[:, 0, :], wr_raw[:], ACT.Copy, scale=scale(ROUTER, S_GU)).then_inc(w_hi, 1)

            def turn(i, j=None, se=None, he=None, le=None, shared_split=None):
                is_first, is_last = isinstance(i, int) and i == 0, isinstance(i, int) and i == B - 1
                n = None if j is None else j * SU

                def square_(k):
                    if se is not None:
                        expert_square(se, k)

                def piece(k):
                    if he is not None:
                        expert_piece(he, k)

                both_exps(i)
                if n is not None and not (isinstance(j, int) and j == 0):
                    unit_hi(n - 1, 1)
                square_(0)
                if n is not None:
                    unit_tanh(n, 0, SHARED)
                if not is_first:
                    second_norm(i - 1)
                square_(1)
                if n is not None:
                    unit_hi(n, 0)
                square_(2)
                if n is not None:
                    unit_tanh(n + 1, 1, SHARED)
                if not (isinstance(i, int) and i < 2):
                    router_out(i - 2)
                if not is_first:
                    act_hi(i - 1)
                if not is_last:
                    first_norm(i + 1)
                if n is not None:
                    unit_hi(n + 1, 1)
                    piece(0)
                    unit_tanh(n + 2, 0, SHARED)
                piece(1)
                piece(2)
                if n is not None:
                    unit_hi(n + 2, 0)
                    piece(3)
                    unit_tanh(n + 3, 1, SHARED)
                piece(4)
                piece(5)
                if is_first:
                    shared_square(0)
                    shared_square(1)
                if shared_split is not None:
                    if shared_split == 0:
                        shared_square(2)
                        shared_square(3)
                    shared_hi(shared_split)
                    shared_hi(shared_split + 1)

            turns(act, turn)

            def shared_tile(j, beside=lambda u: None):
                n = SU * j
                unit_hi(n - 1, 1)
                for u in range(SU):
                    unit_tanh(n + u, u % 2, SHARED)
                    beside(u)
                    if u < SU - 1:
                        unit_hi(n + u, u % 2)

            def last_of_mix(u):
                if u == 0:
                    second_norm(B - 1)
                if u == 1:
                    router_out(B - 2)
                    act_hi(B - 1)
                if u == 2:
                    router_out(B - 1)
                    for k in range(3):
                        expert_square(E - 1, k)
                if u == 3:
                    expert_piece(E - 1, 0)
                    expert_piece(E - 1, 1)

            shared_tile(B - LAG, last_of_mix)

            act.wait_ge(rt, RT_EXP)
            nc.scalar.activation(r_d, r_d, ACT.Exp).then_inc(rt_exp, 1)
            nc.scalar.activation(r_m, r_m, ACT.Exp).then_inc(rt_exp, 1)
            shared_tile(B - LAG + 1, lambda u: expert_piece(E - 1, 2 + u))
            for j in range(B - LAG + 2, B):
                shared_tile(j)

            def gathered_hi(j, r):
                act.wait_ge(g_t, j + 1)
                wait_from(act, gu, N_EXP + j - 1)
                nc.scalar.activation(xe[r][:, 0:H], XT[:], ACT.Copy, scale=XS).then_inc(g_hi, 1)

            def expert_unit(j, r, ahead=True):
                e = act.value_load(span(eidi[0:1, :], j, 1), min_val=0, max_val=E - 1)
                if ahead:
                    gathered_hi(j + 1, 1 - r)
                unit_hi(N_EXP + j - 1, (N_EXP + 1 + r) % 2)
                unit_tanh(N_EXP + j, (N_EXP + r) % 2, e)

            act.wait_ge(rt_pos, 2)
            gathered_hi(0, 0)
            expert_unit(0, 0)
            with act.Fori(0, (NSLOT - 3) // 2) as m:
                expert_unit(m * 2 + 1, 1)
                expert_unit(m * 2 + 2, 0)
            expert_unit(NSLOT - 2, 1)
            expert_unit(NSLOT - 1, 0, ahead=False)
            unit_hi(N_EXP + NSLOT - 1, 0)

        @block.tensor
        def _(pe):
            def transposes(dst, src, n, done):
                for c in range(n):
                    ins = nc.tensor.transpose(dst[:, c * P:(c + 1) * P], src[:, c * P:(c + 1) * P], ident[:])
                ins.then_inc(done, 1)

            def keys_t(t):
                pe.wait_ge(k_rdy, t + 1)
                wait_from(pe, kp1, t)
                transposes(KT, kb, HC, k_t)

            def y_back(t):
                pe.wait_ge(y_rdy, t + 1)
                wait_from(pe, x1_rdy, t)
                transposes(YT, yb, HC, y_t)

            def xn_t_(t):
                pe.wait_ge(xn_rdy, t + 1)
                wait_from(pe, x_lo, t)
                transposes(XT, xnb, HC, xn_t)

            def router(t, sums_before=None):
                pe.wait_ge(x_lo, t + 1)
                if isinstance(t, int) and t == 0:
                    pe.wait_ge(wr_lo, 1)
                wait_from(pe, lg_rdy, t)
                if sums_before is not None:
                    pe.wait_ge(sq_red, sums_before)
                for m in range(3 * HC):
                    c, (xp, wp) = m // 3, HI_LO[m % 3]
                    ins = nc.tensor.matmul(LG[:, 0:RN], span(xt, (t % NX) * (2 * H) + (xp * H + c * P), P),
                                           wr_hl[:, wp, c * RN:(c + 1) * RN], start=m == 0, stop=m == 3 * HC - 1)
                ins.then_inc(logits, 1)

            def sum_squares(k, squares, routed):
                pe.wait_ge(sq, squares)
                wait_from(pe, lg_rdy, routed)
                if isinstance(k, int) and k == 1:
                    nc.tensor.matmul(LG[:, 0:2 * SU], ones[:], ssq[:], start=True, stop=True).then_inc(sq_sum, 1)
                    return
                nc.tensor.matmul(LG[:, 0:2], ones[:], ssqe[:, 0:2], start=True, stop=False)
                nc.tensor.matmul(LG[:, 0:2], ones[:], ssqe[:, 2:4], start=False, stop=True).then_inc(sq_sum, 1)

            def products(par, lhs, base, first, last):
                for m in range(first, last):
                    c, (xp, wp) = m // 3, HI_LO[m % 3]
                    ins = nc.tensor.matmul(GU[par][:], lhs(xp, c), gate_up(base, wp, c), start=m == 0,
                                           stop=m == 3 * HC - 1)
                return ins

            def hidden_t(n, par):
                pe.wait_ge(h_rdy, n + 1)
                wait_from(pe, h_lo, n)
                transposes(HT, hb[par], IC, h_t)

            def down_products(n, par, base, start, stop, sums):
                pe.wait_ge(h_lo, n + 1)
                if start:
                    wait_from(pe, dn_free, sums)
                for m in range(3 * IC):
                    c, (hp, wp) = m // 3, HI_LO[m % 3]
                    ins = nc.tensor.matmul(DN[:], hx[par][:, hp * IE + c * P:hp * IE + (c + 1) * P],
                                           down(base, wp, c), start=start and m == 0, stop=stop and m == 3 * IC - 1)
                ins.then_inc(dn, 1)

            def unit(n, par, lhs, base, before, between=None):
                wait_from(pe, h_rdy, n - 1)
                products(par, lhs, base, 0, 3)
                if between is not None:
                    between()
                products(par, lhs, base, 3, 6)
                if before is not None:
                    down_products(n - 2, par, *before)
                if not (isinstance(n, int) and n == 0):
                    hidden_t(n - 1, 1 - par)
                products(par, lhs, base, 6, 3 * HC).then_inc(gu, 1)

            def shared_down(j, u):
                return sh_base(u), u == 0, u == SU - 1, j

            def shared_units(j, beside=lambda u: None):
                lhs = lambda xp, c: span(xt, (j % NX) * (2 * H) + (xp * H + c * P), P)
                for u in range(SU):
                    if isinstance(j, int) and j == 0:
                        pe.wait_ge(w_lo, u + 1)
                    if u >= 2:
                        before = shared_down(j, u - 2)
                    else:
                        before = None if isinstance(j, int) and j == 0 else shared_down(j - 1, SU - 2 + u)
                    unit(SU * j + u, u % 2, lhs, sh_base(u), before)
                    beside(u)

            pe.wait_ge(consts, CONSTS)
            sum_squares(0, 1, 0)
            keys_t(0)

            def turn(i, j=None, se=None, he=None, le=None, shared_split=None):
                is_first, is_last = isinstance(i, int) and i == 0, isinstance(i, int) and i == B - 1
                if j is None:
                    if not is_first:
                        xn_t_(i - 1)
                    if i >= 2:
                        router(i - 2, 2)
                    keys_t(i + 1)
                    y_back(i)
                    if shared_split == 0:
                        sum_squares(1, 2 * SU + 1, 0)
                else:
                    def beside(u):
                        if u == 0:
                            router(i - 2, E + 1 if se is None else i - 1)
                        if u == 1:
                            xn_t_(i - 1)
                        if u == 2 and se is not None:
                            sum_squares(se + 2, se * 3 + (2 * SU + 4), i - 1)

                    shared_units(j, beside)
                    if not is_last:
                        keys_t(i + 1)
                    y_back(i)

            turns(pe, turn)

            def last_of_mix(u):
                if u == 0:
                    router(B - 2, E + 1)
                if u == 1:
                    xn_t_(B - 1)
                if u == 2:
                    router(B - 1)
                    sum_squares(1 + E, 2 * SU + 1 + 3 * E, B)

            shared_units(B - LAG, last_of_mix)

            def route_sums(u):
                if u > 0:
                    return
                pe.wait_ge(rt, RT_MASK)
                pe.wait_ge(sq_red, E + 2)
                nc.tensor.matmul(KT[:, 0:B * E], tri[:], r_mask, start=True, stop=True)
                nc.tensor.matmul(LG[:, 0:B * E], ones[:], r_mask, start=True, stop=True).then_inc(rt_sums, 1)

            shared_units(B - LAG + 1, route_sums)
            for j in range(B - LAG + 2, B):
                shared_units(j)
            pe.wait_ge(ids_f, 2)
            nc.tensor.transpose(KT[:, 0:NSLOT], ids_float, ident[0:NSLOT, 0:NSLOT])
            nc.tensor.transpose(KT[:, NSLOT:2 * NSLOT], ids_weight, ident[0:NSLOT, 0:NSLOT]).then_inc(ids_t, 1)

            def gathered_t(j, r):
                pe.wait_ge(gather[r], 16 * (j // GATHERS + 1) if isinstance(j, int)
                           else ((j - r) // GATHERS) * 16 + 16)
                wait_from(pe, g_lo, j)
                transposes(XT, xg[r], HC, g_t)

            def expert_of(j):
                return pe.value_load(span(eidi[0:1, :], j, 1), min_val=0, max_val=E - 1) * UW

            def expert_unit(j, r, ahead=True):
                base = expert_of(j)
                if isinstance(j, int) and j < 2:
                    before = shared_down(B - 1, SU - 2 + j)
                else:
                    before = (expert_of(j - 2), True, True, j + (B - 2))
                pe.wait_ge(g_lo, j + 1)
                unit(N_EXP + j, r % 2, lambda xp, c: xe[r % 2][:, xp * H + c * P:xp * H + (c + 1) * P], base, before,
                     (lambda: gathered_t(j + 1, (r + 1) % GATHERS)) if ahead else None)

            pe.wait_ge(w_lo, SU + E)
            pe.wait_ge(rt_pos, 2)
            gathered_t(0, 0)
            for j in range(GATHERS):
                expert_unit(j, j)
            with pe.Fori(1, (NSLOT - GATHERS) // GATHERS + 1) as m:
                for r in range(GATHERS):
                    expert_unit(m * GATHERS + r, r)
            for j in range(NSLOT // GATHERS * GATHERS, NSLOT):
                expert_unit(j, j % GATHERS, ahead=j < NSLOT - 1)
            n = N_EXP + NSLOT
            down_products(n - 2, n % 2, expert_of(NSLOT - 2), True, True, B + NSLOT - 2)
            hidden_t(n - 1, (n - 1) % 2)
            down_products(n - 1, (n - 1) % 2, expert_of(NSLOT - 1), True, True, B + NSLOT - 1)

        @block.vector
        def _(dve):
            TT, STT = nc.vector.tensor_tensor, nc.vector.scalar_tensor_tensor

            def grid(ap):
                return ap.rearrange("p (c t) -> p c t", t=T)

            def keys(t):
                dve.wait_ge(k_t, t + 1)
                wait_from(dve, ymul, t - 1)
                TT(wkv(t, 1), KT[:], growth[:], ALU.subtract).then_inc(kp1, 1)

            def scan_e(t):
                dve.wait_ge(c_ld, t * 16 + 16)
                dve.wait_ge(exps, t + 1)
                TT(wkv(t, 1), wkv(t, 0), part(cb, t), ALU.mult).then_inc(v1, 1)
                dve.wait_ge(v1, t + 1)
                nc.vector.tensor_tensor_scan(wkv(t, 0), decay[:], wkv(t, 0), 0.0, ALU.mult, ALU.add).then_inc(scans, 1)

            def scan_ev(t):
                nc.vector.tensor_tensor_scan(wkv(t, 1), decay[:], wkv(t, 1), 0.0, ALU.mult, ALU.add).then_inc(scans, 1)

            def add_now(t):
                dve.wait_ge(scans, t * 2 + 2)
                dve.wait_ge(v2, t + 1)
                now, before = grid(wkv(t, 2, 2))[:, :, 1:T], grid(wkv(t, 0, 2))[:, :, 0:T - 1]
                TT(now, now, before, ALU.add).then_inc(nd, 1)

            def reciprocals(t, first, n):
                if first == 0:
                    dve.wait_ge(nd, t + 1)
                for c in range(first, first + n):
                    a = wkv_chunk(t, 2, c)
                    nc.vector.reciprocal(a, a).then_inc(rcp, 1)

            def quotient(t):
                dve.wait_ge(rcp, t * HC + HC)
                wait_from(dve, y_t, t)
                if isinstance(t, int) and t == 0:
                    dve.wait_ge(ids_zst, 48)
                TT(yb[:], wkv(t, 3), wkv(t, 2), ALU.mult).then_inc(ymul, 1)
                dve.wait_ge(ymul, t + 1)
                nc.vector.tensor_scalar(grid(yb[:])[:, :, 0:1], grid(part(cb, t))[:, :, 0:1], 1.0, None,
                                        ALU.mult).then_inc(y_rdy, 1)

            def stats(t, k, stat, agg, used):
                plain(dve)
                nc.vector.bn_stats(st6[:, k, :], xrow(t)).then_inc(stat, 1)
                dve.wait_ge(stat, t + 1)
                wait_from(dve, used, t * NORM_STEPS)
                plain(dve)
                nc.vector.bn_aggr(mv[:, k, :], st6[:, k, :]).then_inc(agg, 1)

            def stats1(t):
                dve.wait_ge(x_ld, t * 16 + 16)
                stats(t, 0, stat1, agg1, norm1)

            def residual(t):
                dve.wait_ge(y_t, t + 1)
                TT(xrow(t), YT[:], xrow(t), ALU.add).then_inc(x1_rdy, 1)
                dve.wait_ge(x1_rdy, t + 1)
                stats(t, 1, stat2, agg2, norm2)

            def act_lo(t):
                dve.wait_ge(x_hi, t + 1)
                STT(xt_row(t, 1), XT[:], XS, xt_row(t, 0), ALU.mult, ALU.subtract).then_inc(x_lo, 1)

            def top2_gate(t):
                dve.wait_ge(lg_rdy, t + 1)
                plain(dve)
                nc.vector.max(mx8[:], lgt[:, 0:E]).then_inc(top, 1)
                dve.wait_ge(top, t * TOP_STEPS + 1)
                plain(dve)
                nc.vector.max_index(ix8[:], mx8[:], lgt[:, 0:E]).then_inc(top, 1)
                dve.wait_ge(gate_tanh, t + 1)
                nc.vector.tensor_scalar(span(gate, t, 1), sg[:], 0.5, 0.5, ALU.mult, ALU.add).then_inc(gated, 1)
                nc.vector.tensor_scalar(span(lga, t * E, E), lgt[:, 0:E], 1.0, None, ALU.mult).then_inc(top, 1)
                nc.vector.tensor_scalar(span(mxa, t * TOPK, TOPK), mx8[:, 0:TOPK], 1.0, None,
                                        ALU.mult).then_inc(top, 1)
                dve.wait_ge(top, t * TOP_STEPS + 2)
                nc.vector.tensor_scalar(span(ixa, t * TOPK, TOPK), ix8[:, 0:TOPK], 1.0, None,
                                        ALU.mult).then_inc(top, 1)

            def read_sums(k):
                if not isinstance(k, int) or k > 0:
                    dve.wait_ge(scale_step, k * SCALE_STEPS + 1)
                    plain(dve)
                dve.wait_ge(sq_sum, k + 1)
                plain(dve)
                if isinstance(k, int) and k == 1:
                    ins = nc.vector.tensor_reduce(scw[:], LG[:, 0:2 * SU].rearrange("p (a s) -> p a s", s=SU),
                                                  AX.X, ALU.max)
                else:
                    ins = nc.vector.tensor_copy(scw[:], LG[:, 0:2])
                ins.then_inc(sq_red, 1)
                dve.wait_ge(sq_red, k + 1)
                TS = nc.vector.tensor_scalar
                TS(sci[:, 0:2], scw[:].bitcast(I32), 23, None, ALU.logical_shift_right).then_inc(exponents, 1)
                dve.wait_ge(exponents, k * 3 + 1)
                TS(sci[:, 2:4], sci[:, 0:2], 1, None, ALU.add).then_inc(exponents, 1)
                dve.wait_ge(exponents, k * 3 + 2)
                TS(sci[:, 2:4], sci[:, 2:4], 1, None, ALU.logical_shift_right).then_inc(exponents, 1)

            def shared_lo(s):
                raw, base = (4 + s) * UW, sh_base(s)
                dve.wait_ge(w_hi, 2 * s + 3)
                STT(gate_up(base, 1, 0, HC), span(wall, raw, GUW), scale(SHARED, S_GU), gate_up(base, 0, 0, HC),
                    ALU.mult, ALU.subtract)
                STT(down(base, 1, 0, IC), span(wall, raw + GUW, DW), scale(SHARED, S_D), down(base, 0, 0, IC),
                    ALU.mult, ALU.subtract).then_inc(w_lo, 1)

            def hidden(n, par, row):
                dve.wait_ge(tanh, n + 1)
                STT(th[par][:], th[par][:], 1.0, GU[par][:, 0:IE], ALU.add, ALU.mult).then_inc(a1, 1)
                dve.wait_ge(a1, n + 1)
                wait_from(dve, h_t, n - 1)
                STT(hb[par][:], th[par][:], scale(row, KAPPA), GU[par][:, IE:2 * IE], ALU.mult,
                    ALU.mult).then_inc(h_rdy, 1)

            def hidden_lo(n, par):
                dve.wait_ge(h_hi, n + 1)
                TT(hx[par][:, IE:2 * IE], HT[:, 0:IE], hx[par][:, 0:IE], ALU.subtract).then_inc(h_lo, 1)

            def accumulate(j):
                dve.wait_ge(gated, j * GATE_STEPS + GATE_STEPS)
                dve.wait_ge(scale_step, 2 * SCALE_STEPS + 1)
                TT(gy[:, 0:1], span(gate, j, 1), scale(SHARED, YINV), ALU.mult).then_inc(gyr, 1)
                dve.wait_ge(dn, j * SU + SU)
                dve.wait_ge(gyr, j + 1)
                STT(xrow(j), DN[:], gy[:, 0:1], xrow(j), ALU.mult, ALU.add).then_inc(dn_free, 1)

            dve.wait_ge(consts, CONSTS)
            stats1(0)
            dve.wait_ge(small_ld, 32)
            link = Link(dve, tables)
            w, u = wu_sb[:, 0:HC], wu_sb[:, HC:2 * HC]
            k_ = [wkvc[:, r, :] for r in range(8)]
            link(nc.vector.tensor_scalar(k_[0], w, 0.0, None, ALU.max))
            link(nc.vector.tensor_scalar(k_[1], k_[0], -1.0, None, ALU.mult))
            link(TT(k_[2], u, k_[1], ALU.max))
            link(TT(k_[3], k_[1], k_[2], ALU.subtract))
            link(TT(k_[4], u, k_[0], ALU.add))
            link(nc.vector.tensor_scalar(k_[5], w, 0.0, None, ALU.min))
            assert link.n == WKVC
            dve.wait_ge(tables_act, 2)
            for c in range(HC):
                link(nc.vector.tensor_scalar(growth[:, c * T:(c + 1) * T], decay[:, c * T:(c + 1) * T],
                                             k_[0][:, c:c + 1], k_[3][:, c:c + 1], ALU.mult, ALU.subtract))
            for c in range(HC):
                link(nc.vector.tensor_scalar(decay[:, c * T:(c + 1) * T], decay[:, c * T:(c + 1) * T],
                                             0.0, k_[6][:, c:c + 1], ALU.is_gt, ALU.mult))
            read_sums(0)
            dve.wait_ge(w_hi, 1)
            STT(wr_hl[:, 1, :], wr_raw[:], scale(ROUTER, S_GU), wr_hl[:, 0, :], ALU.mult,
                ALU.subtract).then_inc(wr_lo, 1)

            def turn(i, j=None, se=None, he=None, le=None, shared_split=None):
                is_first, is_last = isinstance(i, int) and i == 0, isinstance(i, int) and i == B - 1
                n = None if j is None else j * SU
                later = n is not None and not (isinstance(j, int) and j == 0)
                keys(i)
                if not is_first:
                    residual(i - 1)
                if not is_last:
                    stats1(i + 1)
                if later:
                    hidden_lo(n - 1, 1)
                scan_e(i)
                if n is not None:
                    hidden(n, 0, SHARED)
                scan_ev(i)
                add_now(i)
                if n is not None:
                    hidden_lo(n, 0)
                if later:
                    accumulate(j - 1)
                if n is not None:
                    hidden(n + 1, 1, SHARED)
                reciprocals(i, 0, 2)
                if n is not None:
                    hidden_lo(n + 1, 1)
                reciprocals(i, 2, 1)
                if n is not None:
                    hidden(n + 2, 0, SHARED)
                reciprocals(i, 3, 1)
                quotient(i)
                if n is not None:
                    hidden_lo(n + 2, 0)
                if n is not None:
                    hidden(n + 3, 1, SHARED)
                if not is_first:
                    act_lo(i - 1)
                if not (isinstance(i, int) and i < 2):
                    top2_gate(i - 2)
                if se is not None:
                    read_sums(se + 2)
                if shared_split is not None:
                    if shared_split == 0:
                        read_sums(1)
                    shared_lo(shared_split)
                    shared_lo(shared_split + 1)

            turns(dve, turn)

            def shared_tile(j, beside=lambda u: None):
                n = SU * j
                hidden_lo(n - 1, 1)
                for u in range(SU):
                    hidden(n + u, u % 2, SHARED)
                    if u == 1:
                        accumulate(j - 1)
                    beside(u)
                    if u < SU - 1:
                        hidden_lo(n + u, u % 2)

            def last_of_mix(u):
                if u == 0:
                    residual(B - 1)
                if u == 1:
                    top2_gate(B - 2)
                    act_lo(B - 1)
                if u == 2:
                    top2_gate(B - 1)
                    read_sums(E + 1)

            shared_tile(B - LAG, last_of_mix)

            step = Link(dve, rt)

            def te(ap):
                return ap.rearrange("p (t e) -> p t e", t=B)

            def et(ap):
                return ap.rearrange("p (e t) -> p e t", e=E)

            def choice(k, buf):
                return buf[:, :].rearrange("p (t k) -> p t k", k=TOPK)[:, :, k:k + 1]

            def route_choices():
                dve.wait_ge(top, TOP_STEPS * B)
                step(TT(te(r_d), te(lga[:]), choice(0, mxa).to_broadcast([P, B, E]), ALU.subtract))
                step(TT(r_m.rearrange("p (t k) -> p t k", k=TOPK), mxa[:, :].rearrange("p (t k) -> p t k", k=TOPK),
                        choice(0, mxa).to_broadcast([P, B, TOPK]), ALU.subtract))
                assert step.n == RT_EXP
                for k, one in enumerate((r_one0, r_one1)):
                    step(TT(te(one), iota8[:].unsqueeze(1).to_broadcast([P, B, E]),
                            choice(k, ixa).to_broadcast([P, B, E]), ALU.is_equal))
                step(TT(r_mask, r_one0, r_one1, ALU.add))
                assert step.n == RT_MASK
                dve.wait_ge(rt_exp, 2)
                step(nc.vector.tensor_reduce(r_sum, te(r_d), AX.X, ALU.add))
                step(nc.vector.reciprocal(r_inv, r_sum))
                for k in range(TOPK):
                    step(TT(pairs[:, k, :, 1:2].bitcast(F32), choice(k, r_m), r_inv.unsqueeze(2), ALU.mult))

            def route_slots():
                dve.wait_ge(rt_sums, 1)
                step(nc.vector.tensor_copy(et(r_tot), LG[:, 0:B * E].rearrange("p (t e) -> p e t", t=B)))
                step(nc.vector.tensor_tensor_scan(r_incl, restart[:], r_tot, 0.0, ALU.mult, ALU.add))
                step(TT(r_tot, r_incl, r_tot, ALU.subtract))
                count = et(r_incl)[:, :, B - 1:B]
                step(nc.vector.tensor_scalar(r_cnt.unsqueeze(2), count, float(P - 1), None, ALU.add))
                step(nc.vector.tensor_scalar(r_cnt, r_cnt, P.bit_length() - 1, None, ALU.logical_shift_right))
                step(nc.vector.tensor_copy(r_tiles, r_cnt))
                step(nc.vector.tensor_tensor_scan(r_end, ones[:, 0:E], r_tiles, 0.0, ALU.mult, ALU.add))
                step(TT(r_off, r_end, r_tiles, ALU.subtract))
                step(STT(et(r_tot), r_off.unsqueeze(2).to_broadcast([P, E, B]), float(P), et(r_tot),
                         ALU.mult, ALU.add))
                step(TT(te(r_pos), KT[:, 0:B * E].rearrange("p (t e) -> p t e", t=B),
                        r_tot.rearrange("p (e t) -> p t e", e=E), ALU.add))
                for k, one in enumerate((r_one0, r_one1)):
                    step(TT(r_prod, r_pos, one, ALU.mult))
                    step(nc.vector.tensor_reduce(r_posf[:, k * B:(k + 1) * B], te(r_prod), AX.X, ALU.add))
                nc.vector.tensor_copy(posi[:, :, :].rearrange("p k t -> p (k t)"), r_posf).then_inc(rt_pos, 1)
                step(TT(r_cmp.rearrange("p (j e) -> p j e", e=E), iotaj[:].unsqueeze(2).to_broadcast([P, NSLOT, E]),
                        r_end.unsqueeze(1).to_broadcast([P, NSLOT, E]), ALU.is_ge))
                step(nc.vector.tensor_reduce(r_eid, r_cmp.rearrange("p (j e) -> p j e", e=E), AX.X, ALU.add))
                nc.vector.tensor_scalar(eidi[:], r_eid, float(E - 1), None, ALU.min).then_inc(rt_pos, 1)

            route_choices()
            shared_tile(B - LAG + 1, lambda u: route_slots() if u == 0 else None)
            for j in range(B - LAG + 2, B):
                shared_tile(j)

            dve.wait_ge(ids_ld, 16)
            nc.vector.tensor_copy(ids_float.unsqueeze(2), ids_back[:, :, 0:1]).then_inc(ids_f, 1)
            nc.vector.tensor_copy(ids_weight.unsqueeze(2), ids_back[:, :, 1:2].bitcast(F32)).then_inc(ids_f, 1)
            dve.wait_ge(ids_t, 1)
            nc.vector.tensor_copy(wsl[:], KT[:, NSLOT:2 * NSLOT]).then_inc(ids_rdy, 1)
            nc.vector.tensor_copy(idsi[:], KT[:, 0:NSLOT]).then_inc(ids_rdy, 1)

            def gathered_lo(j, r):
                dve.wait_ge(g_hi, j + 1)
                STT(xe[r][:, H:2 * H], XT[:], XS, xe[r][:, 0:H], ALU.mult, ALU.subtract).then_inc(g_lo, 1)

            def expert_rows(j, r):
                e = dve.value_load(span(eidi[0:1, :], j, 1), min_val=0, max_val=E - 1)
                if isinstance(j, int) and j < 2:
                    dve.wait_ge(out_st, 16 * B)
                else:
                    dve.wait_ge(added, j * 16 - 16)
                dve.wait_ge(dn, j + (N_EXP + 1))
                nc.vector.tensor_scalar(ye[r], DN[:], scale(e, YINV), span(wsl, j, 1), ALU.mult,
                                        ALU.mult).then_inc(dn_free, 1)

            def expert_unit(j, r, ahead=True):
                e = dve.value_load(span(eidi[0:1, :], j, 1), min_val=0, max_val=E - 1)
                if ahead:
                    gathered_lo(j + 1, 1 - r)
                hidden_lo(N_EXP + j - 1, 1 - r)
                if isinstance(j, int) and j == 1:
                    accumulate(B - 1)
                if not (isinstance(j, int) and j < 2):
                    expert_rows(j - 2, r)
                hidden(N_EXP + j, r, e)

            dve.wait_ge(rt_pos, 2)
            gathered_lo(0, 0)
            for j in range(4):
                expert_unit(j, j % 2)
            with dve.Fori(2, NSLOT // 2) as m:
                expert_unit(m * 2, 0)
                expert_unit(m * 2 + 1, 1)
            expert_unit(NSLOT - 1, 0, ahead=False)
            expert_rows(NSLOT - 2, NSLOT % 2)
            hidden_lo(N_EXP + NSLOT - 1, 0)
            expert_rows(NSLOT - 1, (NSLOT - 1) % 2)


def kernel(**inputs):
    import numpy as np
    from concourse import bacc
    from concourse.bass_utils import run_bass_kernel_spmd

    def halves(gate, up):
        both = np.stack([gate.reshape(-1, IE, HC, P), up.reshape(-1, IE, HC, P)], axis=1)
        return both.transpose(0, 4, 3, 1, 2).reshape(-1, P, GUW)

    def downs(w):
        return w.reshape(-1, H, IC, P).transpose(0, 3, 2, 1).reshape(-1, P, DW)

    a = {n: np.asarray(v) for n, v in inputs.items()}
    ffn = {n[len("L0_ffn_"):]: v for n, v in a.items() if n.startswith("L0_ffn_")}
    wr = np.concatenate([ffn["gate_w"], ffn["shared_expert_gate_w"]], axis=0)
    arrays = {
        "x": a["x"].reshape(B * T, H),
        "ctx_t": a["ctx_2048"].reshape(B, T, HC, P).transpose(0, 3, 2, 1).reshape(B * P, HC * T),
        "wu": np.concatenate([a["L0_xattn_w"].reshape(HC, P).T, a["L0_xattn_u"].reshape(HC, P).T], axis=1),
        "wr": wr.reshape(RN, HC, P).transpose(2, 1, 0).reshape(P, HC * RN),
        "wgu": np.concatenate([halves(ffn["expert_gate_w"], ffn["expert_up_w"]),
                               halves(ffn["shared_gate_w"], ffn["shared_up_w"])], axis=0),
        "wd": np.concatenate([downs(ffn["expert_down_w"]),
                              downs(ffn["shared_down_w"].reshape(H, SU, IE).transpose(1, 0, 2))], axis=0),
    }
    arrays = {n: np.ascontiguousarray(v) for n, v in arrays.items()}
    nc = bacc.Bacc("TRN2", target_bir_lowering=False, num_devices=1)
    aps = {n: nc.dram_tensor(n, v.shape, F32, kind="ExternalInput").ap() for n, v in arrays.items()}
    out = nc.dram_tensor("out", (B * T + P, H), F32, kind="ExternalOutput").ap()
    build(nc, **aps, out=out)
    r = run_bass_kernel_spmd(nc, [arrays], core_ids=[0])
    return r.results[0]["out"][:B * T].reshape(B, T, H)
```

```python
from contextlib import ExitStack

import concourse.bass as bass
from concourse import mybir

F32, F16, I32, U32 = mybir.dt.float32, mybir.dt.float16, mybir.dt.int32, mybir.dt.uint32
ALU, ACT, AX = mybir.AluOpType, mybir.ActivationFunctionType, mybir.AxisListType
ds = bass.ds

P = 128
B, T, H = 16, 128, 512
E, IE, IS, TOPK = 8, 256, 1024, 2
HC = H // P
IC = IE // P
SU = IS // IE
NSLOT = (TOPK * B * T + E * (P - 1)) // P
GUW, DW = HC * 2 * IE, IC * H
UW = GUW + DW
LAG = 2
NX = LAG + 1
NB = 6
SPLIT0 = 1
XS = 1024.0
EPS = 1e-5
RN = E + 1
SHARED, ROUTER = E, E + 1
S_GU, S_D, TANH, KAPPA, YINV = range(5)
HI_LO = [(0, 0), (0, 1), (1, 0)]
WKV0 = E * UW
SH0 = WKV0 + 4 * 2 * H
N_EXP = SU * B
GATHERS = 4
PADS = B * T
LISTS = E * B
XW = H + E
TOP_STEPS, GATE_STEPS, NORM_STEPS, SCALE_STEPS = 5, 1, 4, 10
CONSTS, WKVC = 17, 6
LIST_STEPS, ZEROS, PROBS = 5, 5, 4


def wait_from(eng, sem, value):
    if not (isinstance(value, int) and value <= 0):
        eng.wait_ge(sem, value)


def span(ap, start, n):
    return ap[:, start:start + n] if isinstance(start, int) else ap[:, ds(start, n)]


def rows(dram, t):
    return dram[t * P:(t + 1) * P, :] if isinstance(t, int) else dram[ds(t * P, P), :]


def turns(eng, turn):
    for i in range(SPLIT0):
        turn(i)
    turn(SPLIT0, shared_split=True)
    turn(LAG, j=0, se=0)
    turn(LAG + 1, j=1, se=1, he=0)
    with eng.Fori(LAG + 2, LAG + E - 1) as i:
        turn(i, j=i - LAG, se=i - LAG, he=i - (LAG + 1), le=i - (LAG + 2))
    turn(LAG + E - 1, j=E - 1, he=E - 2, le=E - 3)
    turn(LAG + E, j=E, le=E - 2)
    with eng.Fori(LAG + E + 1, B - 2) as i:
        turn(i, j=i - LAG)
    turn(B - 2, j=B - 2 - LAG)
    turn(B - 1, j=B - 1 - LAG)


class Link:

    def __init__(self, eng, sem):
        self.eng, self.sem, self.n = eng, sem, 0

    def __call__(self, ins):
        self.n += 1
        ins.then_inc(self.sem, 1)
        self.eng.wait_ge(self.sem, self.n)


def build(nc, x, ctx_t, wu, wr, wgu, wd, out):
    ctx = ExitStack()
    with ctx:
        def sb(name, shape, dt=F32):
            return ctx.enter_context(nc.sbuf_tensor(name, shape, dt))

        def bank(name):
            return ctx.enter_context(nc.psum_tensor(name, [P, 512], F32))

        def sems(names):
            return [ctx.enter_context(nc.semaphore(n)) for n in names.split()]

        xn_dram = nc.dram_tensor("xn_rows", (B * T + P, XW), F32).ap()
        ids_dram = nc.dram_tensor("lists", ((LISTS + 1) * P, 1), I32).ap()
        ids_tiles = ids_dram.rearrange("(r p) a -> r (p a)", p=P)

        wall = sb("wall", [P, SH0 + SU * UW])
        wall16 = wall[:, :].bitcast(F16)
        xt = sb("xt", [P, NX * 2 * H], F16)
        xb, cb = sb("xb", [P, NB * XW]), sb("cb", [P, 2 * H])
        kb, yb, xnb = sb("kb", [P, H]), sb("yb", [P, H]), sb("xnb", [P, H])
        growth, decay = sb("growth", [P, HC * T]), sb("decay", [P, HC * T])
        th = [sb(f"th{i}", [P, IE]) for i in range(2)]
        hb = [sb(f"hb{i}", [P, IE]) for i in range(2)]
        hx = [sb(f"hx{i}", [P, 2 * IE], F16) for i in range(2)]
        junk = sb("junk", [P, GUW // 2], mybir.dt.bfloat16)
        ident, ones, tri = sb("ident", [P, P]), sb("ones", [P, P]), sb("tri", [P, P])
        wkvc, wu_sb = sb("wkvc", [P, 8, HC]), sb("wu_sb", [P, 2 * HC])
        wr_raw, wr_hl = sb("wr_raw", [P, HC * RN]), sb("wr_hl", [P, 2, HC * RN], F16)
        st6, mv, nrm = sb("st6", [P, 2, 6]), sb("mv", [P, 2, 2]), sb("nrm", [P, 2, 4])
        mhalf, warm = sb("mhalf", [P, 1]), sb("warm", [P, 1])
        ssq, ssqe = sb("ssq", [P, 2 * SU]), sb("ssqe", [P, 4])
        scw, scf, sci = sb("scw", [P, 2]), sb("scf", [P, 10]), sb("sci", [P, 9], I32)
        scl = sb("scl", [P, (E + 2) * 5])
        lgt, mx8, ix8 = sb("lgt", [P, RN]), sb("mx8", [P, 8]), sb("ix8", [P, 8], U32)
        sg = sb("sg", [P, 1])
        lga, mxa, chosen = sb("lga", [P, B * E]), sb("mxa", [P, B]), sb("chosen", [P, TOPK])
        gate = sb("gate", [P, B])
        ones2, mask, pos2 = sb("ones2", [P, TOPK, E]), sb("mask", [P, E]), sb("pos2", [P, TOPK, E])
        starts, counts, pos = sb("starts", [P, E]), sb("counts", [P, E]), sb("pos", [P, E])
        posf = sb("posf", [P, TOPK])
        posi, toki, listi = sb("posi", [P, TOPK], I32), sb("toki", [P, 1], I32), sb("listi", [P, 1], I32)
        eidi, idsi, wsl = sb("eidi", [P, NSLOT], I32), sb("idsi", [P, NSLOT], I32), sb("wsl", [P, NSLOT])
        idx = [sb(f"idx{i}", [P, 1], I32) for i in range(GATHERS)]
        adx = [sb(f"adx{i}", [P, 1], I32) for i in range(2)]

        iota8, iotaj, iotap = sb("iota8", [P, E]), sb("iotaj", [P, NSLOT]), sb("iotap", [P, 1])
        gy = sb("gy", [P, 2])

        def taken(n, at=[0]):
            at[0] += n
            return cb[:, at[0] - n:at[0]]

        r_d, r_sum, r_inv = taken(B * E), taken(B), taken(B)
        r_cnt, r_tiles, r_end, r_off = taken(E).bitcast(I32), taken(E), taken(E), taken(E)
        r_cmp, r_eid, r_row, r_one, r_of = taken(NSLOT * E), taken(NSLOT), taken(E), taken(E), taken(2)
        ids_back, ids_float = yb[0:NSLOT, 0:P].bitcast(I32), yb[0:NSLOT, P:2 * P]
        late = [(B - NB + k) % NB for k in range(NB)]
        xg = [xb[:, k * XW:(k + 1) * XW] for k in late[0:GATHERS]]
        ye = [xb[:, k * XW:k * XW + H] for k in late[GATHERS:]]
        xe = [kb[:, :].bitcast(F16), xnb[:, :].bitcast(F16)]

        KT, YT, XT, LG = bank("KT"), bank("YT"), bank("XT"), bank("LG")
        GU = [bank("GU0"), bank("GU1")]
        HT, DN = bank("HT"), bank("DN")

        small_ld, x_ld, c_ld, e_ld = sems("small_ld x_ld c_ld e_ld")
        sh_ld, sh_lo = sems("sh_ld0 sh_ld1 sh_ld2 sh_ld3"), sems("sh_lo0 sh_lo1 sh_lo2 sh_lo3")
        xn_st, out_st, added = sems("xn_st out_st added")
        consts, tables, tables_act = sems("consts tables tables_act")
        stat1, agg1, norm1, k_rdy, k_t, kp1, exps, v1, v2 = sems(
            "stat1 agg1 norm1 k_rdy k_t kp1 exps v1 v2")
        scans, nd, rcp, ymul, y_rdy, y_t, x1_rdy, stat2, agg2, norm2 = sems(
            "scans nd rcp ymul y_rdy y_t x1_rdy stat2 agg2 norm2")
        xn_rdy, xn_t, x_hi, x_lo, logits, lg_rdy, gate_tanh, top, gated = sems(
            "xn_rdy xn_t x_hi x_lo logits lg_rdy gate_tanh top gated")
        gu, tanh, a1, h_rdy, h_t, h_hi, h_lo, dn, dn_free = sems("gu tanh a1 h_rdy h_t h_hi h_lo dn dn_free")
        sq, sq_sum, sq_red, exponents, scale_step, w_hi, w_ws, w_lo = sems(
            "sq sq_sum sq_red exponents scale_step w_hi w_ws w_lo")
        token, masked, ranked, listed, probs_st, weighed, rt, rt_exp, rt_pos, ids_zero, ids_zst, scattered, ids_ld, ids_f, ids_t, ids_rdy = sems(
            "token masked ranked listed probs_st weighed rt rt_exp rt_pos ids_zero ids_zst scattered ids_ld ids_f ids_t ids_rdy")
        gather = sems("gather0 gather1 gather2 gather3")
        idx_rdy, adx_rdy, g_t, g_hi, g_lo, wr_lo, gyr, waited = sems(
            "idx_rdy adx_rdy g_t g_hi g_lo wr_lo gyr waited")

        def wkv(t, r, n=1):
            if isinstance(t, int):
                return wall[:, WKV0 + ((t % 2) * 4 + r) * H:WKV0 + ((t % 2) * 4 + r + n) * H]
            return wall[:, ds((t % 2) * (4 * H) + (WKV0 + r * H), n * H)]

        def wkv_chunk(t, r, c):
            off = WKV0 + r * H + c * T
            if isinstance(t, int):
                return wall[:, (t % 2) * 4 * H + off:(t % 2) * 4 * H + off + T]
            return wall[:, ds((t % 2) * (4 * H) + off, T)]

        def part(buf, t):
            return buf[:, (t % 2) * H:(t % 2 + 1) * H] if isinstance(t, int) else buf[:, ds((t % 2) * H, H)]

        def xrow(t):
            return span(xb, (t % NB) * XW, H)

        def xt_row(t, lo):
            return span(xt, (t % NX) * (2 * H) + lo * H, H)

        def split(base, off, n):
            return wall16[:, 2 * base + off:2 * base + off + n] if isinstance(base, int) \
                else wall16[:, ds(base * 2 + off, n)]

        def gate_up(base, lo, c, n=1):
            return split(base, lo * GUW + c * 2 * IE, n * 2 * IE)

        def down(base, lo, c, n=1):
            return split(base, 2 * GUW + lo * DW + c * H, n * H)

        def scale(row, k):
            return span(scl, row * 5 + k, 1)

        def sh_base(s):
            return SH0 + s * UW

        def plain(eng):
            eng.sem_inc(waited, 1)

        block = ctx.enter_context(nc.Block())

        @block.sync
        def _(sp):
            def load_x(t):
                wait_from(sp, out_st, (t - (NB - 1)) * 16)
                plain(sp)
                wait_from(sp, x_ld, t * 16)
                plain(sp)
                sp.dma_start(xrow(t), rows(x, t)).then_inc(x_ld, 16)

            def load_ctx(t):
                wait_from(sp, y_rdy, t - 1)
                plain(sp)
                wait_from(sp, c_ld, t * 16)
                plain(sp)
                sp.dma_start(part(cb, t), rows(ctx_t, t)).then_inc(c_ld, 16)

            def store_xn(t):
                sp.wait_ge(xn_rdy, t + 1)
                plain(sp)
                sp.dma_start(rows(xn_dram, t)[:, 0:H], xnb[:]).then_inc(xn_st, 16)

            def store_sum(j):
                sp.wait_ge(dn_free, j + 1)
                plain(sp)
                wait_from(sp, out_st, j * 16)
                plain(sp)
                sp.dma_start(rows(out, j), xrow(j)).then_inc(out_st, 16)

            def load_expert(e):
                base = (e + 1) * UW
                wait_from(sp, e_ld, e * 32)
                plain(sp)
                if not (isinstance(e, int) and e < 2):
                    for s in range(SU):
                        sp.wait_ge(sh_lo[s], 1)
                src = (wgu[e], wd[e]) if isinstance(e, int) else tuple(
                    w[ds(e, 1), :, :].rearrange("a p n -> (a p) n") for w in (wgu, wd))
                sp.dma_start(span(wall, base, GUW), src[0]).then_inc(e_ld, 16)
                sp.dma_start(span(wall, base + GUW, DW), src[1]).then_inc(e_ld, 16)

            sp.dma_start(wu_sb[:], wu).then_inc(small_ld, 16)
            sp.dma_start(wr_raw[:], wr).then_inc(small_ld, 16)
            load_x(0)
            load_ctx(0)
            sp.wait_ge(ids_zero, 2)
            sp.dma_start(ids_tiles[0:LISTS, :], xnb[:, 0:P].bitcast(I32)).then_inc(ids_zst, 16)
            sp.dma_start(ids_tiles[LISTS:LISTS + 1, :], xnb[0:1, 0:P].bitcast(I32)).then_inc(ids_zst, 16)
            sp.dma_start(xn_dram[PADS:PADS + P, 0:H], yb[:]).then_inc(ids_zst, 16)
            sp.dma_start(xn_dram[PADS:PADS + P, H:XW], yb[:, 0:E]).then_inc(ids_zst, 16)
            sp.dma_start(out[PADS:PADS + P, :], yb[:]).then_inc(ids_zst, 16)
            for s in range(SU):
                sp.dma_start(span(wall, (4 + s) * UW, GUW), wgu[E + s]).then_inc(sh_ld[s], 16)
                sp.dma_start(span(wall, (4 + s) * UW + GUW, DW), wd[E + s]).then_inc(sh_ld[s], 16)
                if s == 0:
                    load_x(1)
                    load_ctx(1)
                    load_x(2)
            load_expert(0)
            load_expert(1)

            def turn(i, j=None, se=None, he=None, le=None, shared_split=False):
                is_first, is_last = isinstance(i, int) and i == 0, isinstance(i, int) and i == B - 1
                if not is_first and not is_last:
                    load_ctx(i + 1)
                if se is not None and not (isinstance(se, int) and se < 2):
                    load_expert(se)
                if not is_first:
                    store_xn(i - 1)
                if j is not None and not (isinstance(j, int) and j == 0):
                    store_sum(j - 1)
                if not (isinstance(i, int) and (i == 0 or i >= B - 2)):
                    load_x(i + 2)

            turns(sp, turn)
            store_xn(B - 1)
            sp.wait_ge(y_rdy, B)
            load_expert(E - 1)
            store_sum(B - LAG - 1)
            sp.wait_ge(rt, PROBS)
            sp.dma_start(xn_dram[0:PADS, H:XW].rearrange("(t p) e -> p t e", p=P),
                         r_d.rearrange("p (t e) -> p t e", e=E)).then_inc(probs_st, 16)
            for j in range(B - LAG, B - 1):
                store_sum(j)
            store_sum(B - 1)
            sp.wait_ge(out_st, 16 * B)
            sp.wait_ge(added, 16 * NSLOT)

        @block.gpsimd
        def _(pool):
            link = Link(pool, consts)
            pool.memset(yb[:], 0.0).then_inc(ids_zero, 1)
            pool.iota(xnb[:, 0:P].bitcast(I32), [[1, P]], base=PADS, channel_multiplier=0).then_inc(ids_zero, 1)
            for buf in (ssq, ssqe, scf, sci):
                link(pool.memset(buf[:], 0))
            link(pool.memset(mhalf[:], -0.5))
            link(pool.memset(ones[:], 1.0))
            link(pool.memset(ident[:], 0.0))
            link(pool.affine_select(out=ident[:], in_=ident[:], compare_op=ALU.not_equal, fill=1.0,
                                    base=0, pattern=[[-1, P]], channel_multiplier=1))
            link(pool.affine_select(out=tri[:], in_=ones[:], compare_op=ALU.is_gt, fill=0.0,
                                    base=0, pattern=[[1, P]], channel_multiplier=-1))
            link(pool.iota(decay[:], [[0, HC], [1, T]], base=0, channel_multiplier=0,
                           allow_small_or_imprecise_dtypes=True))
            link(pool.iota(toki[:], [[0, 1]], base=0, channel_multiplier=1))
            for buf, pattern, channel in ((iota8, [[1, E]], 0), (iotaj, [[1, NSLOT]], 0), (iotap, [[0, 1]], 1),
                                          (starts, [[B * T, E]], 0), (counts, [[B * T, E]], 0)):
                link(pool.iota(buf[:], pattern, base=0, channel_multiplier=channel,
                               allow_small_or_imprecise_dtypes=True))
            link(pool.memset(warm[:], 0.0))
            assert link.n == CONSTS

            def norm(t, k, stats_rdy, steps, used):
                pool.wait_ge(stats_rdy, t + 1)
                wait_from(pool, used, t)
                plain(pool)
                nc.gpsimd.tensor_scalar(nrm[:, k, 0:1], mv[:, k, 1:2], EPS, None, ALU.add).then_inc(steps, 1)
                nc.gpsimd.tensor_scalar(nrm[:, k, 1:2], mv[:, k, 0:1], -1.0, None, ALU.mult).then_inc(steps, 1)
                pool.wait_ge(steps, t * NORM_STEPS + 2)
                nc.gpsimd.tensor_tensor(nrm[:, k, 2:3], nrm[:, k, 0:1], mhalf[:], ALU.pow).then_inc(steps, 1)
                pool.wait_ge(steps, t * NORM_STEPS + 3)
                nc.gpsimd.tensor_tensor(nrm[:, k, 3:4], nrm[:, k, 1:2], nrm[:, k, 2:3], ALU.mult).then_inc(steps, 1)

            def second_product(t):
                pool.wait_ge(c_ld, t * 16 + 16)
                pool.wait_ge(exps, t + 1)
                nc.gpsimd.tensor_tensor(wkv(t, 3), wkv(t, 2), part(cb, t), ALU.mult).then_inc(v2, 1)

            def expert_lo(e, k):
                raw = (e + 1) * UW + k * (GUW // 2)
                hi, lo = (gate_up(e * UW, q, 0, HC) if k < 2 else down(e * UW, q, 0, IC) for q in range(2))
                if k == 0:
                    pool.wait_ge(w_ws, e * 3 + 3)
                if k < 2:
                    half = GUW // 2
                    hi, lo = split(e * UW, k * half, half), split(e * UW, GUW + k * half, half)
                ins = nc.gpsimd.tensor_tensor(lo, span(wall, raw, GUW // 2), hi, ALU.subtract)
                if k == 2:
                    ins.then_inc(w_lo, 1)

            def scales(k, row):
                base = 0 if isinstance(k, int) and k == 0 else k * SCALE_STEPS + 1
                TS, n = nc.gpsimd.tensor_scalar, 0

                def step(ins, wait=True):
                    nonlocal n
                    n += 1
                    ins.then_inc(scale_step, 1)
                    if wait:
                        pool.wait_ge(scale_step, base + n)
                        plain(pool)

                pool.wait_ge(exponents, k * 3 + 3)
                plain(pool)
                field = [scf[:, 4 + f:5 + f] for f in range(5)]
                e_gu, e_d, h_gu, h_d, tmp = (scf[:, c:c + 1] for c in (0, 1, 2, 3, 9))
                step(TS(scf[:, 0:4], sci[:, 0:4], 1.0, None, ALU.mult))
                step(TS(scf[:, 4:6], scf[:, 2:4], -1.0, 205.0, ALU.mult, ALU.add), False)
                step(TS(field[TANH], h_gu, 38.0, None, ALU.add), False)
                step(TS(tmp, h_gu, 2.0, 83.0, ALU.mult, ALU.add), False)
                step(TS(field[YINV], e_gu, -84.0, None, ALU.add))
                step(nc.gpsimd.tensor_tensor(field[KAPPA], tmp, e_gu, ALU.subtract), False)
                step(nc.gpsimd.tensor_tensor(field[YINV], field[YINV], h_d, ALU.add))
                step(TS(field[YINV], field[YINV], 0.0, 254.0, ALU.max, ALU.min))
                step(TS(sci[:, 4:9], scf[:, 4:9], float(1 << 23), None, ALU.mult))
                step(pool.tensor_copy(span(scl, row * 5, 5).bitcast(I32), sci[:, 4:9]))
                assert n == SCALE_STEPS

            norm(0, 0, agg1, norm1, k_rdy)
            def scatter(t):
                if isinstance(t, int) and t == 0:
                    pool.wait_ge(ids_zst, ZEROS * 16)
                else:
                    pool.wait_ge(scattered, t * (TOPK * 16))
                    plain(pool)
                    pool.tensor_scalar(toki[:], toki[:], P, None, ALU.add).then_inc(token, 1)
                    pool.wait_ge(token, t)
                    plain(pool)
                pool.wait_ge(listed, t * LIST_STEPS + LIST_STEPS)
                plain(pool)
                for k in range(TOPK):
                    pool.indirect_dma_start(ids_dram, bass.IndirectOffsetOnAxis(ap=posi[:, k:k + 1], axis=0),
                                            toki[:], None).then_inc(scattered, 16)

            scales(0, ROUTER)
            nc.gpsimd.tensor_scalar(scale(ROUTER, YINV), scale(ROUTER, TANH), 2.0, None,
                                    ALU.mult).then_inc(scale_step, 1)

            def turn(i, j=None, se=None, he=None, le=None, shared_split=False):
                if not (isinstance(i, int) and i == 0):
                    norm(i - 1, 1, agg2, norm2, xn_rdy)
                if not (isinstance(i, int) and i == B - 1):
                    norm(i + 1, 0, agg1, norm1, k_rdy)
                second_product(i)
                if le is not None:
                    for k in range(3):
                        expert_lo(le, k)
                if se is not None:
                    scales(se + 2, se)
                if not (isinstance(i, int) and i < 3):
                    scatter(i - 3)
                if shared_split:
                    scales(1, SHARED)

            turns(pool, turn)
            norm(B - 1, 1, agg2, norm2, xn_rdy)
            for t in range(B - 3, B):
                scatter(t)
            scales(E + 1, E - 1)
            pool.wait_ge(scattered, TOPK * B * 16)
            pool.wait_ge(rt_pos, 2)
            pool.indirect_dma_start(ids_back, None, ids_tiles,
                                    bass.IndirectOffsetOnAxis(ap=listi[0:NSLOT, 0:1], axis=0)).then_inc(ids_ld, 16)

            pool.wait_ge(ids_rdy, 1)
            pool.wait_ge(xn_st, 16 * B)
            pool.wait_ge(probs_st, 16)
            pool.wait_ge(out_st, 16 * (B - 2))

            def gather_tile(j, r):
                if not isinstance(j, int):
                    pool.wait_ge(gather[r], (j - r) // GATHERS * 16)
                elif j >= GATHERS:
                    pool.wait_ge(gather[r], j // GATHERS * 16)
                pool.tensor_copy(idx[r][:], span(idsi, j, 1)).then_inc(idx_rdy, 1)
                wait_from(pool, weighed, j - GATHERS + 1)
                plain(pool)
                pool.wait_ge(idx_rdy, j + 1)
                plain(pool)
                pool.indirect_dma_start(xg[r], None, xn_dram, bass.IndirectOffsetOnAxis(ap=idx[r][:, 0:1], axis=0)
                                        ).then_inc(gather[r], 16)

            def add_rows(j, r):
                wait_from(pool, added, j * 16)
                plain(pool)
                pool.tensor_copy(adx[r][:], span(idsi, j, 1)).then_inc(adx_rdy, 1)
                pool.wait_ge(dn_free, j + (B + 1))
                plain(pool)
                pool.wait_ge(adx_rdy, j + 1)
                plain(pool)
                pool.indirect_dma_start(out, bass.IndirectOffsetOnAxis(ap=adx[r][:, 0:1], axis=0), ye[r], None,
                                        compute_op=ALU.add).then_inc(added, 16)

            for j in range(GATHERS + 1):
                gather_tile(j, j % GATHERS)
            pool.wait_ge(out_st, 16 * B)
            for j in range(GATHERS + 1, 2 * GATHERS):
                gather_tile(j, j % GATHERS)
                add_rows(j - (GATHERS + 1), (j + 1) % 2)
            with pool.Fori(2, (NSLOT - GATHERS) // GATHERS + 1) as m:
                for r in range(GATHERS):
                    gather_tile(m * GATHERS + r, r)
                    add_rows(m * GATHERS + (r - (GATHERS + 1)), (r + 1) % 2)
            for j in range(NSLOT // GATHERS * GATHERS, NSLOT):
                gather_tile(j, j % GATHERS)
                add_rows(j - (GATHERS + 1), (j + 1) % 2)
            for j in range(NSLOT - (GATHERS + 1), NSLOT):
                add_rows(j, j % 2)

        @block.scalar
        def _(act):
            def square(src, junk, n, out1):
                nc.scalar.activation(junk, src, ACT.Square, accum_out=out1).then_inc(sq, 1)

            act.wait_ge(consts, CONSTS)
            nc.scalar.activation(warm[:], mhalf[:], ACT.Tanh).then_inc(tables_act, 1)
            act.wait_ge(tables, WKVC)
            nc.scalar.activation(wkvc[:, 6, :], wkvc[:, 5, :], ACT.Exp).then_inc(tables_act, 1)
            act.wait_ge(small_ld, 32)
            square(wr_raw[:], junk[:, 0:HC * RN], HC * RN, ssqe[:, 0:1])

            def first_norm(t):
                act.wait_ge(norm1, (t + 1) * NORM_STEPS)
                wait_from(act, k_t, t)
                plain(act)
                nc.scalar.activation(kb[:], xrow(t), ACT.Identity, bias=nrm[:, 0, 3:4],
                                     scale=nrm[:, 0, 2:3]).then_inc(k_rdy, 1)

            def second_norm(t):
                act.wait_ge(norm2, (t + 1) * NORM_STEPS)
                wait_from(act, xn_t, t)
                wait_from(act, xn_st, 16 * t)
                if isinstance(t, int) and t == 0:
                    act.wait_ge(ids_zst, ZEROS * 16)
                plain(act)
                nc.scalar.activation(xnb[:], xrow(t), ACT.Identity, bias=nrm[:, 1, 3:4],
                                     scale=nrm[:, 1, 2:3]).then_inc(xn_rdy, 1)

            def both_exps(t):
                act.wait_ge(kp1, t + 1)
                wait_from(act, ymul, t - 1)
                plain(act)
                for c in range(HC):
                    nc.scalar.activation(wkv_chunk(t, 2, c), wkv_chunk(t, 1, c), ACT.Exp, bias=wkvc[:, 4, c:c + 1])
                nc.scalar.activation(wkv(t, 0), wkv(t, 1), ACT.Exp).then_inc(exps, 1)

            def act_hi(t):
                act.wait_ge(xn_t, t + 1)
                if not isinstance(t, int) or t >= NX:
                    act.wait_ge(gu, (t - NX + 1) * SU)
                plain(act)
                nc.scalar.activation(xt_row(t, 0), XT[:], ACT.Copy, scale=XS).then_inc(x_hi, 1)

            def router_out(t):
                act.wait_ge(logits, t + 1)
                wait_from(act, top, t * TOP_STEPS)
                nc.scalar.activation(lgt[:], LG[:, 0:RN], ACT.Copy, scale=scale(ROUTER, YINV)).then_inc(lg_rdy, 1)
                act.wait_ge(lg_rdy, t + 1)
                wait_from(act, gated, t * GATE_STEPS)
                nc.scalar.activation(sg[:], lgt[:, E:E + 1], ACT.Tanh, scale=0.5).then_inc(gate_tanh, 1)

            def unit_tanh(n, par, row):
                act.wait_ge(gu, n + 1)
                wait_from(act, h_rdy, n - 1)
                plain(act)
                nc.scalar.activation(th[par][:], GU[par][:, 0:IE], ACT.Tanh, scale=scale(row, TANH)).then_inc(tanh, 1)

            def unit_hi(n, par):
                act.wait_ge(h_t, n + 1)
                wait_from(act, dn, n - 1)
                nc.scalar.activation(hx[par][:, 0:IE], HT[:, 0:IE], ACT.Copy).then_inc(h_hi, 1)

            def shared_square(s):
                act.wait_ge(sh_ld[s], 32)
                wait_from(act, sq_sum, 1)
                raw = (4 + s) * UW
                square(span(wall, raw, GUW), span(wall, sh_base(s), GUW), GUW, ssq[:, s:s + 1])
                square(span(wall, raw + GUW, DW), span(wall, sh_base(s) + GUW, DW), DW, ssq[:, SU + s:SU + s + 1])

            def shared_hi(s):
                raw = (4 + s) * UW
                act.wait_ge(scale_step, 2 * SCALE_STEPS + 1)
                nc.scalar.activation(gate_up(sh_base(s), 0, 0, HC), span(wall, raw, GUW), ACT.Copy,
                                     scale=scale(SHARED, S_GU)).then_inc(w_hi, 1)
                nc.scalar.activation(down(sh_base(s), 0, 0, IC), span(wall, raw + GUW, DW), ACT.Copy,
                                     scale=scale(SHARED, S_D)).then_inc(w_hi, 1)

            def expert_square(e, k):
                if k == 0:
                    act.wait_ge(e_ld, (e + 1) * 32)
                    plain(act)
                    act.wait_ge(sq_sum, e + 2)
                act.wait_ge(sq, e * 3 + (2 * SU + 1 + k))
                plain(act)
                n = GUW // 2
                square(span(wall, (e + 1) * UW + k * n, n), junk[:], n, ssqe[:, (0, 2, 1)[k]:(0, 2, 1)[k] + 1])

            def expert_piece(e, k):
                half = GUW // 2
                raw = span(wall, (e + 1) * UW + k % 3 * half, half)
                if k == 0:
                    act.wait_ge(scale_step, e * SCALE_STEPS + (3 * SCALE_STEPS + 1))
                    plain(act)
                    wait_from(act, w_lo, e)
                    plain(act)
                if k < 3:
                    hi = split(e * UW, k * half, half) if k < 2 else down(e * UW, 0, 0, IC)
                    nc.scalar.activation(hi, raw, ACT.Copy, scale=scale(e, S_GU if k < 2 else S_D)).then_inc(w_hi, 1)
                else:
                    act.wait_ge(w_hi, e * 3 + (2 * SU + 2 + k - 3))
                    plain(act)
                    nc.scalar.activation(raw, raw, ACT.Copy, scale=scale(e, S_GU if k < 5 else S_D)).then_inc(w_ws, 1)

            first_norm(0)
            act.wait_ge(scale_step, SCALE_STEPS + 1)
            nc.scalar.activation(wr_hl[:, 0, :], wr_raw[:], ACT.Copy, scale=scale(ROUTER, S_GU)).then_inc(w_hi, 1)

            shared_square(0)

            def turn(i, j=None, se=None, he=None, le=None, shared_split=False):
                is_first, is_last = isinstance(i, int) and i == 0, isinstance(i, int) and i == B - 1
                n = None if j is None else j * SU

                def square_(k):
                    if se is not None:
                        expert_square(se, k)

                def piece(k):
                    if he is not None:
                        expert_piece(he, k)

                both_exps(i)
                if is_first:
                    shared_square(1)
                    shared_square(2)
                if n is not None and not (isinstance(j, int) and j == 0):
                    unit_hi(n - 1, 1)
                square_(0)
                if n is not None:
                    unit_tanh(n, 0, SHARED)
                if not is_first:
                    second_norm(i - 1)
                square_(1)
                if n is not None:
                    unit_hi(n, 0)
                square_(2)
                if n is not None:
                    unit_tanh(n + 1, 1, SHARED)
                if not (isinstance(i, int) and i < 2):
                    router_out(i - 2)
                if not is_first:
                    act_hi(i - 1)
                if not is_last:
                    first_norm(i + 1)
                if n is not None:
                    unit_hi(n + 1, 1)
                    piece(0)
                    unit_tanh(n + 2, 0, SHARED)
                piece(1)
                piece(2)
                if n is not None:
                    unit_hi(n + 2, 0)
                    piece(3)
                    unit_tanh(n + 3, 1, SHARED)
                piece(4)
                piece(5)
                if is_first:
                    shared_square(3)
                if shared_split:
                    for s in range(SU):
                        shared_hi(s)

            turns(act, turn)

            def shared_tile(j, beside=lambda u: None):
                n = SU * j
                unit_hi(n - 1, 1)
                for u in range(SU):
                    unit_tanh(n + u, u % 2, SHARED)
                    beside(u)
                    if u < SU - 1:
                        unit_hi(n + u, u % 2)

            def last_of_mix(u):
                if u == 0:
                    second_norm(B - 1)
                if u == 1:
                    router_out(B - 2)
                    act_hi(B - 1)
                if u == 2:
                    router_out(B - 1)

            def last_expert(u):
                if u == 0:
                    for k in range(3):
                        expert_square(E - 1, k)
                if u == 3:
                    for k in range(3):
                        expert_piece(E - 1, k)

            shared_tile(B - LAG, last_of_mix)
            act.wait_ge(rt, 1)
            nc.scalar.activation(r_d, r_d, ACT.Exp).then_inc(rt_exp, 1)
            shared_tile(B - LAG + 1, last_expert)

            def gathered_hi(j, r):
                act.wait_ge(g_t, j + 1)
                wait_from(act, gu, N_EXP + j - 1)
                nc.scalar.activation(xe[r][:, 0:H], XT[:], ACT.Copy, scale=XS).then_inc(g_hi, 1)

            def expert_unit(j, r, ahead=True):
                e = act.value_load(span(eidi[0:1, :], j, 1), min_val=0, max_val=E - 1)
                if ahead:
                    gathered_hi(j + 1, 1 - r)
                unit_hi(N_EXP + j - 1, (N_EXP + 1 + r) % 2)
                unit_tanh(N_EXP + j, (N_EXP + r) % 2, e)

            act.wait_ge(rt_pos, 2)
            gathered_hi(0, 0)
            expert_unit(0, 0)
            with act.Fori(0, (NSLOT - 3) // 2) as m:
                expert_unit(m * 2 + 1, 1)
                expert_unit(m * 2 + 2, 0)
            expert_unit(NSLOT - 2, 1)
            expert_unit(NSLOT - 1, 0, ahead=False)
            unit_hi(N_EXP + NSLOT - 1, 0)

        @block.tensor
        def _(pe):
            def transposes(dst, src, n, done):
                for c in range(n):
                    ins = nc.tensor.transpose(dst[:, c * P:(c + 1) * P], src[:, c * P:(c + 1) * P], ident[:])
                ins.then_inc(done, 1)

            def keys_t(t):
                pe.wait_ge(k_rdy, t + 1)
                wait_from(pe, kp1, t)
                transposes(KT, kb, HC, k_t)

            def y_back(t):
                pe.wait_ge(y_rdy, t + 1)
                wait_from(pe, x1_rdy, t)
                transposes(YT, yb, HC, y_t)

            def xn_t_(t):
                pe.wait_ge(xn_rdy, t + 1)
                wait_from(pe, x_lo, t)
                transposes(XT, xnb, HC, xn_t)

            def router(t, sums_before=None):
                pe.wait_ge(x_lo, t + 1)
                if isinstance(t, int) and t == 0:
                    pe.wait_ge(wr_lo, 1)
                wait_from(pe, lg_rdy, t)
                if sums_before is not None:
                    pe.wait_ge(sq_red, sums_before)
                for m in range(3 * HC):
                    c, (xp, wp) = m // 3, HI_LO[m % 3]
                    ins = nc.tensor.matmul(LG[:, 0:RN], span(xt, (t % NX) * (2 * H) + (xp * H + c * P), P),
                                           wr_hl[:, wp, c * RN:(c + 1) * RN], start=m == 0, stop=m == 3 * HC - 1)
                ins.then_inc(logits, 1)

            def sum_squares(k, squares, routed):
                pe.wait_ge(sq, squares)
                wait_from(pe, lg_rdy, routed)
                wait_from(pe, sq_red, k)
                if isinstance(k, int) and k == 1:
                    nc.tensor.matmul(LG[:, 0:2 * SU], ones[:], ssq[:], start=True, stop=True).then_inc(sq_sum, 1)
                    return
                nc.tensor.matmul(LG[:, 0:2], ones[:], ssqe[:, 0:2], start=True, stop=False)
                nc.tensor.matmul(LG[:, 0:2], ones[:], ssqe[:, 2:4], start=False, stop=True).then_inc(sq_sum, 1)

            def ranks(t):
                pe.wait_ge(masked, t * 2 + 2)
                pe.wait_ge(lg_rdy, t + 2 if not isinstance(t, int) else min(t + 2, B))
                nc.tensor.matmul(LG[:, 16:16 + E], tri[:], mask[:], start=True, stop=True)
                nc.tensor.matmul(LG[:, 16 + E:16 + 2 * E], ones[:], mask[:], start=True, stop=True).then_inc(ranked, 1)

            def products(par, lhs, base, first, last):
                for m in range(first, last):
                    c, (xp, wp) = m // 3, HI_LO[m % 3]
                    ins = nc.tensor.matmul(GU[par][:], lhs(xp, c), gate_up(base, wp, c), start=m == 0,
                                           stop=m == 3 * HC - 1)
                return ins

            def hidden_t(n, par):
                pe.wait_ge(h_rdy, n + 1)
                wait_from(pe, h_lo, n)
                transposes(HT, hb[par], IC, h_t)

            def down_products(n, par, base, start, stop, sums):
                pe.wait_ge(h_lo, n + 1)
                if start:
                    wait_from(pe, dn_free, sums)
                for m in range(3 * IC):
                    c, (hp, wp) = m // 3, HI_LO[m % 3]
                    ins = nc.tensor.matmul(DN[:], hx[par][:, hp * IE + c * P:hp * IE + (c + 1) * P],
                                           down(base, wp, c), start=start and m == 0, stop=stop and m == 3 * IC - 1)
                ins.then_inc(dn, 1)

            def unit(n, par, lhs, base, before, between=None):
                wait_from(pe, h_rdy, n - 1)
                products(par, lhs, base, 0, 3)
                if between is not None:
                    between()
                products(par, lhs, base, 3, 6)
                if before is not None:
                    down_products(n - 2, par, *before)
                if not (isinstance(n, int) and n == 0):
                    hidden_t(n - 1, 1 - par)
                products(par, lhs, base, 6, 3 * HC).then_inc(gu, 1)

            def shared_down(j, u):
                return sh_base(u), u == 0, u == SU - 1, j

            def shared_units(j, beside=lambda u: None):
                lhs = lambda xp, c: span(xt, (j % NX) * (2 * H) + (xp * H + c * P), P)
                pe.wait_ge(x_lo, j + 1)
                for u in range(SU):
                    if isinstance(j, int) and j == 0:
                        pe.wait_ge(sh_lo[u], 1)
                    if u >= 2:
                        before = shared_down(j, u - 2)
                    else:
                        before = None if isinstance(j, int) and j == 0 else shared_down(j - 1, SU - 2 + u)
                    unit(SU * j + u, u % 2, lhs, sh_base(u), before)
                    beside(u)

            pe.wait_ge(consts, CONSTS)
            sum_squares(0, 1, 0)
            keys_t(0)

            def turn(i, j=None, se=None, he=None, le=None, shared_split=False):
                is_first, is_last = isinstance(i, int) and i == 0, isinstance(i, int) and i == B - 1
                if j is None:
                    if not is_first:
                        xn_t_(i - 1)
                    keys_t(i + 1)
                    y_back(i)
                    if is_first:
                        sum_squares(1, 2 * SU + 1, 0)
                else:
                    def beside(u):
                        if u == 0:
                            if not (isinstance(i, int) and i < 4):
                                pe.wait_ge(listed, (i - 4) * LIST_STEPS + 2)
                            router(i - 2, E + 1 if se is None else i + (2 - LAG))
                        if u == 1:
                            xn_t_(i - 1)
                        if u == 2 and not (isinstance(i, int) and i < 3):
                            ranks(i - 3)
                        if u == 2 and se is not None:
                            sum_squares(se + 2, se * 3 + (2 * SU + 4), i - 1)

                    shared_units(j, beside)
                    if not is_last:
                        keys_t(i + 1)
                    y_back(i)

            turns(pe, turn)

            def last_of_mix(u):
                if u == 0:
                    pe.wait_ge(listed, (B - 4) * LIST_STEPS + 2)
                    router(B - 2, E + 1)
                if u == 1:
                    xn_t_(B - 1)
                    ranks(B - 3)
                if u == 2:
                    pe.wait_ge(listed, (B - 3) * LIST_STEPS + 2)
                    router(B - 1)
                    ranks(B - 2)

            def last_sums(u):
                if u == 0:
                    ranks(B - 1)
                if u == 1:
                    pe.wait_ge(listed, (B - 1) * LIST_STEPS + 2)
                    sum_squares(1 + E, 2 * SU + 1 + 3 * E, B)

            shared_units(B - LAG, last_of_mix)
            shared_units(B - LAG + 1, last_sums)
            pe.wait_ge(ids_f, 1)
            nc.tensor.transpose(KT[:, 0:NSLOT], ids_float, ident[0:NSLOT, 0:NSLOT]).then_inc(ids_t, 1)

            def gathered_t(j, r):
                pe.wait_ge(gather[r], 16 * (j // GATHERS + 1) if isinstance(j, int)
                           else ((j - r) // GATHERS) * 16 + 16)
                wait_from(pe, g_lo, j)
                transposes(XT, xg[r], HC, g_t)

            def expert_of(j):
                return pe.value_load(span(eidi[0:1, :], j, 1), min_val=0, max_val=E - 1) * UW

            def expert_unit(j, r, ahead=True):
                base = expert_of(j)
                if isinstance(j, int) and j < 2:
                    before = shared_down(B - 1, SU - 2 + j)
                else:
                    before = (expert_of(j - 2), True, True, j + (B - 2))
                pe.wait_ge(g_lo, j + 1)
                unit(N_EXP + j, r % 2, lambda xp, c: xe[r % 2][:, xp * H + c * P:xp * H + (c + 1) * P], base, before,
                     (lambda: gathered_t(j + 1, (r + 1) % GATHERS)) if ahead else None)

            pe.wait_ge(w_lo, E)
            pe.wait_ge(rt_pos, 2)
            gathered_t(0, 0)
            for j in range(GATHERS):
                expert_unit(j, j)
            with pe.Fori(1, (NSLOT - GATHERS) // GATHERS + 1) as m:
                for r in range(GATHERS):
                    expert_unit(m * GATHERS + r, r)
            for j in range(NSLOT // GATHERS * GATHERS, NSLOT):
                expert_unit(j, j % GATHERS, ahead=j < NSLOT - 1)
            n = N_EXP + NSLOT
            down_products(n - 2, n % 2, expert_of(NSLOT - 2), True, True, B + NSLOT - 2)
            hidden_t(n - 1, (n - 1) % 2)
            down_products(n - 1, (n - 1) % 2, expert_of(NSLOT - 1), True, True, B + NSLOT - 1)

        @block.vector
        def _(dve):
            TT, STT = nc.vector.tensor_tensor, nc.vector.scalar_tensor_tensor

            def grid(ap):
                return ap.rearrange("p (c t) -> p c t", t=T)

            def keys(t):
                dve.wait_ge(k_t, t + 1)
                wait_from(dve, ymul, t - 1)
                TT(wkv(t, 1), KT[:], growth[:], ALU.subtract).then_inc(kp1, 1)

            def scan_e(t):
                dve.wait_ge(c_ld, t * 16 + 16)
                dve.wait_ge(exps, t + 1)
                TT(wkv(t, 1), wkv(t, 0), part(cb, t), ALU.mult).then_inc(v1, 1)
                dve.wait_ge(v1, t + 1)
                nc.vector.tensor_tensor_scan(wkv(t, 0), decay[:], wkv(t, 0), 0.0, ALU.mult, ALU.add).then_inc(scans, 1)

            def scan_ev(t):
                nc.vector.tensor_tensor_scan(wkv(t, 1), decay[:], wkv(t, 1), 0.0, ALU.mult, ALU.add).then_inc(scans, 1)

            def add_now(t):
                dve.wait_ge(scans, t * 2 + 2)
                dve.wait_ge(v2, t + 1)
                now, before = grid(wkv(t, 2, 2))[:, :, 1:T], grid(wkv(t, 0, 2))[:, :, 0:T - 1]
                TT(now, now, before, ALU.add).then_inc(nd, 1)

            def reciprocals(t, first, n):
                if first == 0:
                    dve.wait_ge(nd, t + 1)
                for c in range(first, first + n):
                    a = wkv_chunk(t, 2, c)
                    nc.vector.reciprocal(a, a).then_inc(rcp, 1)

            def quotient(t):
                dve.wait_ge(rcp, t * HC + HC)
                wait_from(dve, y_t, t)
                if isinstance(t, int) and t == 0:
                    dve.wait_ge(ids_zst, ZEROS * 16)
                TT(yb[:], wkv(t, 3), wkv(t, 2), ALU.mult).then_inc(ymul, 1)
                dve.wait_ge(ymul, t + 1)
                nc.vector.tensor_scalar(grid(yb[:])[:, :, 0:1], grid(part(cb, t))[:, :, 0:1], 1.0, None,
                                        ALU.mult).then_inc(y_rdy, 1)

            def stats(t, k, stat, agg, used):
                plain(dve)
                nc.vector.bn_stats(st6[:, k, :], xrow(t)).then_inc(stat, 1)
                dve.wait_ge(stat, t + 1)
                wait_from(dve, used, t * NORM_STEPS)
                plain(dve)
                nc.vector.bn_aggr(mv[:, k, :], st6[:, k, :]).then_inc(agg, 1)

            def stats1(t):
                dve.wait_ge(x_ld, t * 16 + 16)
                stats(t, 0, stat1, agg1, norm1)

            def residual(t):
                dve.wait_ge(y_t, t + 1)
                TT(xrow(t), YT[:], xrow(t), ALU.add).then_inc(x1_rdy, 1)
                dve.wait_ge(x1_rdy, t + 1)
                stats(t, 1, stat2, agg2, norm2)

            def act_lo(t):
                dve.wait_ge(x_hi, t + 1)
                STT(xt_row(t, 1), XT[:], XS, xt_row(t, 0), ALU.mult, ALU.subtract).then_inc(x_lo, 1)

            def top2_gate(t):
                dve.wait_ge(lg_rdy, t + 1)
                plain(dve)
                nc.vector.max(mx8[:], lgt[:, 0:E]).then_inc(top, 1)
                dve.wait_ge(top, t * TOP_STEPS + 1)
                plain(dve)
                nc.vector.max_index(ix8[:], mx8[:], lgt[:, 0:E]).then_inc(top, 1)
                dve.wait_ge(gate_tanh, t + 1)
                nc.vector.tensor_scalar(span(gate, t, 1), sg[:], 0.5, 0.5, ALU.mult, ALU.add).then_inc(gated, 1)
                nc.vector.tensor_scalar(span(lga, t * E, E), lgt[:, 0:E], 1.0, None, ALU.mult).then_inc(top, 1)
                nc.vector.tensor_scalar(span(mxa, t, 1), mx8[:, 0:1], 1.0, None, ALU.mult).then_inc(top, 1)
                dve.wait_ge(top, t * TOP_STEPS + 2)
                wait_from(dve, masked, t * 2)
                nc.vector.tensor_scalar(chosen[:], ix8[:, 0:TOPK], 1.0, None, ALU.mult).then_inc(top, 1)

            def choices(t):
                dve.wait_ge(top, t * TOP_STEPS + TOP_STEPS)
                wait_from(dve, listed, t * LIST_STEPS)
                TT(ones2[:], iota8[:].unsqueeze(1).to_broadcast([P, TOPK, E]),
                   chosen[:].unsqueeze(2).to_broadcast([P, TOPK, E]), ALU.is_equal).then_inc(masked, 1)
                dve.wait_ge(masked, t * 2 + 1)
                TT(mask[:], ones2[:, 0, :], ones2[:, 1, :], ALU.add).then_inc(masked, 1)

            def places(t):
                dve.wait_ge(ranked, t + 1)
                TT(pos[:], counts[:], LG[:, 16:16 + E], ALU.add).then_inc(listed, 1)
                dve.wait_ge(listed, t * LIST_STEPS + 1)
                TT(counts[:], counts[:], LG[:, 16 + E:16 + 2 * E], ALU.add).then_inc(listed, 1)
                TT(pos2[:], ones2[:], pos[:].unsqueeze(1).to_broadcast([P, TOPK, E]), ALU.mult).then_inc(listed, 1)
                dve.wait_ge(listed, t * LIST_STEPS + 3)
                nc.vector.tensor_reduce(posf[:], pos2[:], AX.X, ALU.add).then_inc(listed, 1)
                dve.wait_ge(listed, t * LIST_STEPS + 4)
                wait_from(dve, scattered, t * (TOPK * 16))
                nc.vector.tensor_scalar(posi[:], posf[:], 1.0, None, ALU.mult).then_inc(listed, 1)

            def read_sums(k):
                if not isinstance(k, int) or k > 0:
                    dve.wait_ge(scale_step, k * SCALE_STEPS + 1)
                    plain(dve)
                dve.wait_ge(sq_sum, k + 1)
                plain(dve)
                if isinstance(k, int) and k == 1:
                    ins = nc.vector.tensor_reduce(scw[:], LG[:, 0:2 * SU].rearrange("p (a s) -> p a s", s=SU),
                                                  AX.X, ALU.max)
                else:
                    ins = nc.vector.tensor_copy(scw[:], LG[:, 0:2])
                ins.then_inc(sq_red, 1)
                dve.wait_ge(sq_red, k + 1)
                TS = nc.vector.tensor_scalar
                TS(sci[:, 0:2], scw[:].bitcast(I32), 23, None, ALU.logical_shift_right).then_inc(exponents, 1)
                dve.wait_ge(exponents, k * 3 + 1)
                TS(sci[:, 2:4], sci[:, 0:2], 1, None, ALU.add).then_inc(exponents, 1)
                dve.wait_ge(exponents, k * 3 + 2)
                TS(sci[:, 2:4], sci[:, 2:4], 1, None, ALU.logical_shift_right).then_inc(exponents, 1)

            def shared_lo(s):
                raw, base = (4 + s) * UW, sh_base(s)
                dve.wait_ge(w_hi, 2 * s + 3)
                STT(gate_up(base, 1, 0, HC), span(wall, raw, GUW), scale(SHARED, S_GU), gate_up(base, 0, 0, HC),
                    ALU.mult, ALU.subtract)
                STT(down(base, 1, 0, IC), span(wall, raw + GUW, DW), scale(SHARED, S_D), down(base, 0, 0, IC),
                    ALU.mult, ALU.subtract).then_inc(sh_lo[s], 1)

            def last_expert_lo():
                e = E - 1
                dve.wait_ge(w_hi, 2 * SU + 1 + 3 * E)
                STT(gate_up(e * UW, 1, 0, HC), span(wall, (e + 1) * UW, GUW), scale(e, S_GU),
                    gate_up(e * UW, 0, 0, HC), ALU.mult, ALU.subtract)
                STT(down(e * UW, 1, 0, IC), span(wall, (e + 1) * UW + GUW, DW), scale(e, S_D),
                    down(e * UW, 0, 0, IC), ALU.mult, ALU.subtract).then_inc(w_lo, 1)

            def hidden(n, par, row):
                dve.wait_ge(tanh, n + 1)
                STT(th[par][:], th[par][:], 1.0, GU[par][:, 0:IE], ALU.add, ALU.mult).then_inc(a1, 1)
                dve.wait_ge(a1, n + 1)
                wait_from(dve, h_t, n - 1)
                STT(hb[par][:], th[par][:], scale(row, KAPPA), GU[par][:, IE:2 * IE], ALU.mult,
                    ALU.mult).then_inc(h_rdy, 1)

            def hidden_lo(n, par):
                dve.wait_ge(h_hi, n + 1)
                TT(hx[par][:, IE:2 * IE], HT[:, 0:IE], hx[par][:, 0:IE], ALU.subtract).then_inc(h_lo, 1)

            def accumulate(j):
                dve.wait_ge(gated, j * GATE_STEPS + GATE_STEPS)
                dve.wait_ge(scale_step, 2 * SCALE_STEPS + 1)
                TT(gy[:, 0:1], span(gate, j, 1), scale(SHARED, YINV), ALU.mult).then_inc(gyr, 1)
                dve.wait_ge(dn, j * SU + SU)
                dve.wait_ge(gyr, j + 1)
                STT(xrow(j), DN[:], gy[:, 0:1], xrow(j), ALU.mult, ALU.add).then_inc(dn_free, 1)

            dve.wait_ge(consts, CONSTS)
            stats1(0)
            dve.wait_ge(small_ld, 32)
            link = Link(dve, tables)
            w, u = wu_sb[:, 0:HC], wu_sb[:, HC:2 * HC]
            k_ = [wkvc[:, r, :] for r in range(8)]
            link(nc.vector.tensor_scalar(k_[0], w, 0.0, None, ALU.max))
            link(nc.vector.tensor_scalar(k_[1], k_[0], -1.0, None, ALU.mult))
            link(TT(k_[2], u, k_[1], ALU.max))
            link(TT(k_[3], k_[1], k_[2], ALU.subtract))
            link(TT(k_[4], u, k_[0], ALU.add))
            link(nc.vector.tensor_scalar(k_[5], w, 0.0, None, ALU.min))
            assert link.n == WKVC
            dve.wait_ge(tables_act, 2)
            for c in range(HC):
                link(nc.vector.tensor_scalar(growth[:, c * T:(c + 1) * T], decay[:, c * T:(c + 1) * T],
                                             k_[0][:, c:c + 1], k_[3][:, c:c + 1], ALU.mult, ALU.subtract))
            for c in range(HC):
                link(nc.vector.tensor_scalar(decay[:, c * T:(c + 1) * T], decay[:, c * T:(c + 1) * T],
                                             0.0, k_[6][:, c:c + 1], ALU.is_gt, ALU.mult))
            read_sums(0)
            dve.wait_ge(w_hi, 1)
            STT(wr_hl[:, 1, :], wr_raw[:], scale(ROUTER, S_GU), wr_hl[:, 0, :], ALU.mult,
                ALU.subtract).then_inc(wr_lo, 1)

            def turn(i, j=None, se=None, he=None, le=None, shared_split=False):
                is_first, is_last = isinstance(i, int) and i == 0, isinstance(i, int) and i == B - 1
                n = None if j is None else j * SU
                later = n is not None and not (isinstance(j, int) and j == 0)
                keys(i)
                if not is_first:
                    residual(i - 1)
                if not is_last:
                    stats1(i + 1)
                if not (isinstance(i, int) and i < 3):
                    choices(i - 3)
                if shared_split:
                    read_sums(1)
                if later:
                    hidden_lo(n - 1, 1)
                scan_e(i)
                if n is not None:
                    hidden(n, 0, SHARED)
                scan_ev(i)
                add_now(i)
                if n is not None:
                    hidden_lo(n, 0)
                if later:
                    accumulate(j - 1)
                if n is not None:
                    hidden(n + 1, 1, SHARED)
                reciprocals(i, 0, 2)
                if n is not None:
                    hidden_lo(n + 1, 1)
                reciprocals(i, 2, 1)
                if n is not None:
                    hidden(n + 2, 0, SHARED)
                reciprocals(i, 3, 1)
                quotient(i)
                if n is not None:
                    hidden_lo(n + 2, 0)
                if not is_first:
                    act_lo(i - 1)
                if not (isinstance(i, int) and i < 2):
                    top2_gate(i - 2)
                if n is not None:
                    hidden(n + 3, 1, SHARED)
                if se is not None:
                    read_sums(se + 2)
                if not (isinstance(i, int) and i < 3):
                    places(i - 3)
                if shared_split:
                    for s in range(SU):
                        shared_lo(s)

            turns(dve, turn)

            def shared_tile(j, beside=lambda u: None):
                n = SU * j
                hidden_lo(n - 1, 1)
                for u in range(SU):
                    hidden(n + u, u % 2, SHARED)
                    if u == 1:
                        accumulate(j - 1)
                    beside(u)
                    if u < SU - 1:
                        hidden_lo(n + u, u % 2)

            def last_of_mix(u):
                if u == 0:
                    residual(B - 1)
                    choices(B - 3)
                if u == 1:
                    top2_gate(B - 2)
                    act_lo(B - 1)
                    places(B - 3)
                    choices(B - 2)
                if u == 2:
                    places(B - 2)
                    top2_gate(B - 1)
                if u == 3:
                    choices(B - 1)
                    probabilities()

            step = Link(dve, rt)

            def probabilities():
                r3 = r_d.rearrange("p (t e) -> p t e", e=E)
                dve.wait_ge(top, TOP_STEPS * B)
                step(TT(r3, lga[:, :].rearrange("p (t e) -> p t e", e=E),
                        mxa[:].unsqueeze(2).to_broadcast([P, B, E]), ALU.subtract))
                dve.wait_ge(rt_exp, 1)
                step(nc.vector.tensor_reduce(r_sum, r3, AX.X, ALU.add))
                step(nc.vector.reciprocal(r_inv, r_sum))
                step(TT(r3, r3, r_inv.unsqueeze(2).to_broadcast([P, B, E]), ALU.mult))
                assert step.n == PROBS

            def tiles_of_lists():
                TS = nc.vector.tensor_scalar
                dve.wait_ge(listed, LIST_STEPS * B)
                step(TT(r_one, counts[:], starts[:], ALU.subtract))
                step(TS(r_cnt, r_one, float(P - 1), None, ALU.add))
                step(TS(r_cnt, r_cnt, P.bit_length() - 1, None, ALU.logical_shift_right))
                step(nc.vector.tensor_copy(r_tiles, r_cnt))
                step(nc.vector.tensor_tensor_scan(r_end, ones[:, 0:E], r_tiles, 0.0, ALU.mult, ALU.add))
                step(TT(r_off, r_end, r_tiles, ALU.subtract))
                step(TS(r_one, r_end, iotap[:], None, ALU.is_le))
                step(nc.vector.tensor_reduce(r_of[:, 0:1], r_one, AX.X, ALU.add))
                step(TS(r_of[:, 0:1], r_of[:, 0:1], float(E - 1), None, ALU.min))
                step(TS(r_one, iota8[:], r_of[:, 0:1], None, ALU.is_equal))
                step(STT(r_row, iota8[:], float(B), r_off, ALU.mult, ALU.subtract))
                step(TT(r_row, r_row, r_one, ALU.mult))
                step(nc.vector.tensor_reduce(r_of[:, 1:2], r_row, AX.X, ALU.add))
                step(TS(listi[:], r_of[:, 1:2], iotap[:], float(LISTS), ALU.add, ALU.min))
                step(TT(r_cmp.rearrange("p (j e) -> p j e", e=E), iotaj[:].unsqueeze(2).to_broadcast([P, NSLOT, E]),
                        r_end.unsqueeze(1).to_broadcast([P, NSLOT, E]), ALU.is_ge))
                step(nc.vector.tensor_reduce(r_eid, r_cmp.rearrange("p (j e) -> p j e", e=E), AX.X, ALU.add))
                TS(eidi[:], r_eid, float(E - 1), None, ALU.min).then_inc(rt_pos, 2)

            shared_tile(B - LAG, last_of_mix)

            def route_ends(u):
                if u == 0:
                    places(B - 1)
                if u == 1:
                    tiles_of_lists()
                if u == 2:
                    read_sums(E + 1)

            shared_tile(B - LAG + 1, route_ends)
            last_expert_lo()

            dve.wait_ge(ids_ld, 16)
            nc.vector.tensor_copy(ids_float, ids_back).then_inc(ids_f, 1)
            dve.wait_ge(ids_t, 1)
            nc.vector.tensor_copy(idsi[:], KT[:, 0:NSLOT]).then_inc(ids_rdy, 1)

            def gathered_lo(j, r):
                dve.wait_ge(g_hi, j + 1)
                STT(xe[r][:, H:2 * H], XT[:], XS, xe[r][:, 0:H], ALU.mult, ALU.subtract).then_inc(g_lo, 1)

            def expert_rows(j, r):
                e = dve.value_load(span(eidi[0:1, :], j, 1), min_val=0, max_val=E - 1)
                if isinstance(j, int) and j < 2:
                    dve.wait_ge(out_st, 16 * B)
                else:
                    dve.wait_ge(added, j * 16 - 16)
                dve.wait_ge(weighed, j + 1)
                dve.wait_ge(dn, j + (N_EXP + 1))
                nc.vector.tensor_scalar(ye[r], DN[:], scale(e, YINV), span(wsl, j, 1), ALU.mult,
                                        ALU.mult).then_inc(dn_free, 1)

            def expert_unit(j, q, ahead=True):
                r = q % 2
                e = dve.value_load(span(eidi[0:1, :], j, 1), min_val=0, max_val=E - 1)
                if ahead:
                    gathered_lo(j + 1, 1 - r)
                hidden_lo(N_EXP + j - 1, 1 - r)
                nc.vector.tensor_scalar(span(wsl, j, 1), span(xg[q], e + H, 1), 1.0, None, ALU.mult).then_inc(weighed, 1)
                if isinstance(j, int) and j == 1:
                    accumulate(B - 1)
                if not (isinstance(j, int) and j < 2):
                    expert_rows(j - 2, r)
                hidden(N_EXP + j, r, e)

            dve.wait_ge(rt_pos, 2)
            gathered_lo(0, 0)
            for j in range(GATHERS):
                expert_unit(j, j)
            with dve.Fori(1, (NSLOT - GATHERS) // GATHERS + 1) as m:
                for q in range(GATHERS):
                    expert_unit(m * GATHERS + q, q)
            for j in range(NSLOT // GATHERS * GATHERS, NSLOT):
                expert_unit(j, j % GATHERS, ahead=j < NSLOT - 1)
            expert_rows(NSLOT - 2, NSLOT % 2)
            hidden_lo(N_EXP + NSLOT - 1, 0)
            expert_rows(NSLOT - 1, (NSLOT - 1) % 2)


def kernel(**inputs):
    import numpy as np
    from concourse import bacc
    from concourse.bass_utils import run_bass_kernel_spmd

    def halves(gate, up):
        both = np.stack([gate.reshape(-1, IE, HC, P), up.reshape(-1, IE, HC, P)], axis=1)
        return both.transpose(0, 4, 3, 1, 2).reshape(-1, P, GUW)

    def downs(w):
        return w.reshape(-1, H, IC, P).transpose(0, 3, 2, 1).reshape(-1, P, DW)

    a = {n: np.asarray(v) for n, v in inputs.items()}
    ffn = {n[len("L0_ffn_"):]: v for n, v in a.items() if n.startswith("L0_ffn_")}
    wr = np.concatenate([ffn["gate_w"], ffn["shared_expert_gate_w"]], axis=0)
    arrays = {
        "x": a["x"].reshape(B * T, H),
        "ctx_t": a["ctx_2048"].reshape(B, T, HC, P).transpose(0, 3, 2, 1).reshape(B * P, HC * T),
        "wu": np.concatenate([a["L0_xattn_w"].reshape(HC, P).T, a["L0_xattn_u"].reshape(HC, P).T], axis=1),
        "wr": wr.reshape(RN, HC, P).transpose(2, 1, 0).reshape(P, HC * RN),
        "wgu": np.concatenate([halves(ffn["expert_gate_w"], ffn["expert_up_w"]),
                               halves(ffn["shared_gate_w"], ffn["shared_up_w"])], axis=0),
        "wd": np.concatenate([downs(ffn["expert_down_w"]),
                              downs(ffn["shared_down_w"].reshape(H, SU, IE).transpose(1, 0, 2))], axis=0),
    }
    arrays = {n: np.ascontiguousarray(v) for n, v in arrays.items()}
    nc = bacc.Bacc("TRN2", target_bir_lowering=False, num_devices=1)
    aps = {n: nc.dram_tensor(n, v.shape, F32, kind="ExternalInput").ap() for n, v in arrays.items()}
    out = nc.dram_tensor("out", (B * T + P, H), F32, kind="ExternalOutput").ap()
    build(nc, **aps, out=out)
    r = run_bass_kernel_spmd(nc, [arrays], core_ids=[0])
    return r.results[0]["out"][:B * T].reshape(B, T, H)
```
